# Optimizing a Trainium2 kernel written in Bass

```python
import numpy as np
import jax
import jax.numpy as jnp

def _softmax(x, axis=-1):
    return jax.nn.softmax(x, axis=axis)

def _gelu(x):
    return jax.nn.gelu(x, approximate=True)

def _silu(x):
    return jax.nn.silu(x)

def _sigmoid(x):
    return jax.nn.sigmoid(x)

def _layernorm(x, axis=-1, eps=1e-05):
    m = jnp.mean(x, axis=axis, keepdims=True)
    v = jnp.var(x, axis=axis, keepdims=True)
    return (x - m) / jnp.sqrt(v + eps)

def _scatter_add(tgt, idx, src, axis=0):
    return tgt.at[idx].add(src)

def _segment_sum(src, seg, n):
    return jax.ops.segment_sum(src, seg, n)
kernel_name = 'mk_prb_d1_jaxref_r8_40f6f4'

def setup_inputs(seed: int=0):
    np.random.seed(seed)
    _w = jnp.asarray

    def _L0_attn_setup():
        import jax, jax.numpy as jnp
        import numpy as np
        import math
        B, S, E = (2, 256, 256)
        H, KVH = (32, 8)
        D = E // H
        THETA, SCALE = (10000.0, 1.0)

        def _rope_cos_sin(seq_len, dim):
            inv_freq = 1.0 / THETA ** (jnp.arange(0, dim, 2, dtype=jnp.float32) / dim)
            t = jnp.arange(seq_len, dtype=jnp.float32) / SCALE
            freqs = jnp.outer(t, inv_freq)
            emb = jnp.concatenate([freqs, freqs], -1)
            return (jnp.cos(emb)[None, :, None, :], jnp.sin(emb)[None, :, None, :])

        def _rotate_half(x):
            d = x.shape[-1] // 2
            return jnp.concatenate([-x[..., d:], x[..., :d]], axis=-1)

        def _apply_rope(x, cos, sin):
            return x * cos + _rotate_half(x) * sin
        key = jax.random.key(seed)
        ks = jax.random.split(key, 5)
        sc = 0.02
        return {'x': jax.random.normal(ks[0], (B, S, E), jnp.float32), 'Wq': jax.random.normal(ks[1], (E, E), jnp.float32) * sc, 'Wk': jax.random.normal(ks[2], (KVH * D, E), jnp.float32) * sc, 'Wv': jax.random.normal(ks[3], (KVH * D, E), jnp.float32) * sc, 'Wo': jax.random.normal(ks[4], (E, E), jnp.float32) * sc}
    _L0_attn_in = _L0_attn_setup()

    def _L0_ffn_setup():
        import jax, jax.numpy as jnp
        import numpy as np
        E = 8
        TOP_K = 2
        D = 256
        F = 128
        FS = 256
        B, T = (2, 128)
        key = jax.random.key(seed)
        ks = jax.random.split(key, 8)
        s = 0.02
        return {'x': jax.random.normal(ks[0], (B, T, D), dtype=jnp.float32), 'router_w': jax.random.normal(ks[1], (D, E), dtype=jnp.float32) * s, 'shared_gate': jax.random.normal(ks[2], (D, FS), dtype=jnp.float32) * s, 'shared_up': jax.random.normal(ks[3], (D, FS), dtype=jnp.float32) * s, 'shared_down': jax.random.normal(ks[4], (FS, D), dtype=jnp.float32) * s, 'w_gate': jax.random.normal(ks[5], (E, D, F), dtype=jnp.float32) * s, 'w_up': jax.random.normal(ks[6], (E, D, F), dtype=jnp.float32) * s, 'w_down': jax.random.normal(ks[7], (E, F, D), dtype=jnp.float32) * s}
    _L0_ffn_in = _L0_ffn_setup()
    _d = {'L0_attn_x': _L0_attn_in['x'], 'L0_attn_Wq': _L0_attn_in['Wq'], 'L0_attn_Wk': _L0_attn_in['Wk'], 'L0_attn_Wv': _L0_attn_in['Wv'], 'L0_attn_Wo': _L0_attn_in['Wo'], 'L0_ffn_router_w': _L0_ffn_in['router_w'], 'L0_ffn_shared_gate': _L0_ffn_in['shared_gate'], 'L0_ffn_shared_up': _L0_ffn_in['shared_up'], 'L0_ffn_shared_down': _L0_ffn_in['shared_down'], 'L0_ffn_w_gate': _L0_ffn_in['w_gate'], 'L0_ffn_w_up': _L0_ffn_in['w_up'], 'L0_ffn_w_down': _L0_ffn_in['w_down']}
    _x0 = _d['L0_attn_x']
    _d['L0_attn_x'] = jax.random.normal(jax.random.fold_in(jax.random.key(seed), 1), (2, 1024, 256), dtype=_x0.dtype)
    del _x0
    return _d

def reference(L0_attn_x, L0_attn_Wq, L0_attn_Wk, L0_attn_Wv, L0_attn_Wo, L0_ffn_router_w, L0_ffn_shared_gate, L0_ffn_shared_up, L0_ffn_shared_down, L0_ffn_w_gate, L0_ffn_w_up, L0_ffn_w_down):

    def _L0_attn_ref(x, Wq, Wk, Wv, Wo):
        import jax, jax.numpy as jnp
        import numpy as np
        import math
        B, S, E = (2, 256, 256)
        H, KVH = (32, 8)
        D = E // H
        THETA, SCALE = (10000.0, 1.0)

        def _rope_cos_sin(seq_len, dim):
            inv_freq = 1.0 / THETA ** (jnp.arange(0, dim, 2, dtype=jnp.float32) / dim)
            t = jnp.arange(seq_len, dtype=jnp.float32) / SCALE
            freqs = jnp.outer(t, inv_freq)
            emb = jnp.concatenate([freqs, freqs], -1)
            return (jnp.cos(emb)[None, :, None, :], jnp.sin(emb)[None, :, None, :])

        def _rotate_half(x):
            d = x.shape[-1] // 2
            return jnp.concatenate([-x[..., d:], x[..., :d]], axis=-1)

        def _apply_rope(x, cos, sin):
            return x * cos + _rotate_half(x) * sin
        b, s, _ = x.shape
        Q = (x @ Wq.T).reshape(b, s, H, D)
        K = (x @ Wk.T).reshape(b, s, KVH, D)
        V = (x @ Wv.T).reshape(b, s, KVH, D)
        cos, sin = _rope_cos_sin(s, D)
        Q = _apply_rope(Q, cos, sin)
        K = _apply_rope(K, cos, sin)
        rep = H // KVH
        K = jnp.repeat(K, rep, axis=2)
        V = jnp.repeat(V, rep, axis=2)
        scores = jnp.einsum('bqhd,bkhd->bhqk', Q, K) / math.sqrt(D)
        probs = jax.nn.softmax(scores, axis=-1)
        out = jnp.einsum('bhqk,bkhd->bqhd', probs, V).reshape(b, s, H * D)
        return out @ Wo.T

    def _L0_ffn_ref(x, router_w, shared_gate, shared_up, shared_down, w_gate, w_up, w_down):
        import jax, jax.numpy as jnp
        import numpy as np
        E = 8
        TOP_K = 2
        D = 256
        F = 128
        FS = 256
        B, T = (2, 128)
        Bx, Tx, Dx = x.shape
        N = Bx * Tx
        xf = x.reshape(N, Dx)
        shared = jax.nn.silu(xf @ shared_gate) * (xf @ shared_up) @ shared_down
        probs = jax.nn.softmax(xf @ router_w, axis=-1)
        topk_vals, topk_ids = jax.lax.top_k(probs, TOP_K)
        combine = jnp.zeros((N, E), dtype=xf.dtype).at[jnp.arange(N)[:, None], topk_ids].add(topk_vals)
        gated = jax.nn.silu(jnp.einsum('nd,edf->enf', xf, w_gate))
        up = jnp.einsum('nd,edf->enf', xf, w_up)
        y = jnp.einsum('enf,efd->end', gated * up, w_down)
        routed = jnp.einsum('ne,end->nd', combine, y)
        return (shared + routed).reshape(Bx, Tx, Dx)
    x = L0_attn_x
    xn = _layernorm(x, axis=-1)
    x = x + _L0_attn_ref(xn, L0_attn_Wq, L0_attn_Wk, L0_attn_Wv, L0_attn_Wo) + _L0_ffn_ref(xn, L0_ffn_router_w, L0_ffn_shared_gate, L0_ffn_shared_up, L0_ffn_shared_down, L0_ffn_w_gate, L0_ffn_w_up, L0_ffn_w_down)
    return x

_drawn_inputs = setup_inputs


def setup_inputs(seed=0):
    import zlib

    import numpy as np

    out = dict(_drawn_inputs(seed))
    spreads = {}
    factors = {'L0_attn_Wq': 8.0,
     'L0_attn_Wk': 8.0,
     'L0_attn_Wv': 8.0,
     'L0_attn_Wo': 8.0,
     'L0_ffn_router_w': 8.0,
     'L0_ffn_shared_gate': 3.371,
     'L0_ffn_shared_up': 3.324,
     'L0_ffn_shared_down': 3.324,
     'L0_ffn_w_gate': 8.0,
     'L0_ffn_w_up': 8.0,
     'L0_ffn_w_down': 8.0}
    for name, (base, spread) in spreads.items():
        noise = np.random.default_rng([zlib.crc32(name.encode()), seed]).standard_normal(out[name].shape)
        drawn = base * np.exp(spread * noise) if base else spread * noise
        out[name] = jnp.asarray(drawn.astype(out[name].dtype))
    for name, factor in factors.items():
        out[name] = (out[name] * factor).astype(out[name].dtype)
    return out
```

```python
from contextlib import ExitStack

import numpy as np

import concourse.bass as bass
from concourse import mybir

ALU = mybir.AluOpType
ACT = mybir.ActivationFunctionType
AX = mybir.AxisListType
F32 = mybir.dt.float32
BF16 = mybir.dt.bfloat16

P = 128
B, S, E = 2, 1024, 256
H, KV = 32, 8
D = E // H
REP = H // KV
N = B * S
KE = E // P
BLK = 512
NBLK = N // BLK
TB = BLK // P
NT = N // P
EXP = 8
FT = 2 + EXP
EPS = 1e-5
HALF = D // 2

QPART = (0, 0, 0, 1, 1, 2)
KPART = (0, 1, 2, 0, 1, 0)
NP = len(QPART)
SR = NP * D
MR = 3
SH = 64

G = B * KV
KT = S // P
QH = S // BLK
STEPS = QH * KT
UNITS = REP * (S // P) * (S // BLK)
UPS = UNITS // STEPS
LEAD = 4
AHEAD = UNITS + LEAD * UPS
ROT = 4
LSTEPS = 2 * STEPS
TURNS = (G * STEPS - ROT) // LSTEPS
PSLOTS = 8
VW = 32
SCALE = 1.0 / float(np.sqrt(D))
LAG = 3
HSLOTS = 5
FROT = HSLOTS


def ffn_attention_block(nc, x, wqkv, wo, wgu, wdn, wvr, tables, out):
    ctx = ExitStack()
    with ctx:
        def sb(name, shape, dt=F32):
            return ctx.enter_context(nc.sbuf_tensor(name, shape, dt))

        def sem(name):
            return ctx.enter_context(nc.semaphore(name))

        bank = [ctx.enter_context(nc.psum_tensor(f"bank{n}", [P, 2 * BLK], F32)) for n in range(4)]

        def pb(n):
            return bank[n // 2][:, (n % 2) * BLK:(n % 2 + 1) * BLK]

        q_stacks = nc.dram_tensor("q_stacks", (G, REP, NP, D, S), BF16).ap()
        k_stacks = nc.dram_tensor("k_stacks", (G, NP, D, S), BF16).ap()
        weights_by_expert = nc.dram_tensor("weights_by_expert", (EXP, N), F32).ap()
        max_rows = nc.dram_tensor("max_rows", (2, 2, 2, MR, S), BF16).ap()
        heads_out = nc.dram_tensor("heads_out", (G, REP, D + 1, S), F32).ap()

        res = sb("res", [P, NT, E])
        xn = sb("xn", [P, NT, E])
        xnT = sb("xnT", [P, KE, N])
        w_gu = sb("w_gu", [P, KE, FT, 2, P])
        w_dn = sb("w_dn", [P, FT, E])
        w_o = sb("w_o", [P, KE, E])
        w_qk = sb("w_qk", [P, KE, 2, 2 * P + SH])
        w_vr = sb("w_vr", [P, KE, KV * D + EXP])
        cos_sin = sb("cos_sin", [P, 2, S])
        ident = sb("ident", [P, P])
        zeros = sb("zeros", [P, P])
        before = sb("before", [P, EXP * EXP])
        hid = sb("hid", [P, HSLOTS, BLK])
        mix = sb("mix", [P, EXP, BLK])
        parts = sb("parts", [P, 2, 3, BLK], BF16)
        q1 = sb("q1", [P, 2, 2, S], BF16)
        k1 = sb("k1", [P, 2, S], BF16)
        q2 = sb("q2", [P, 2, 2, S], BF16)
        k2 = sb("k2", [P, 2, S], BF16)
        probs = sb("probs", [P, PSLOTS, 2 * BLK])
        heads = sb("heads", [P, 2, BLK])
        v_all = sb("v_all", [P, B, KV, KT, D])
        v_now = sb("v_now", [P, 2, KT, VW])
        stats = sb("stats", [P, NT, 6])
        mv = sb("mv", [P, NT, 2])
        ln = sb("ln", [P, 4, NT])
        logits = sb("logits", [P, NT, EXP])
        rt = sb("rt", [P, 2, NT, EXP])
        rs = sb("rs", [P, 2, NT])
        rank = sb("rank", [P, 2, NT, EXP, EXP])
        comb = sb("comb", [P, EXP, NT])
        combT = sb("combT", [P, P])
        unit_max = sb("unit_max", [P, 2, UNITS])
        neg_max = sb("neg_max", [P, 2, UNITS // 2])
        neg_maxT = sb("neg_maxT", [REP * KT, P])
        neg_rest = sb("neg_rest", [REP * KT, P])
        neg_parts = sb("neg_parts", [REP * KT, MR, P], BF16)
        xflat = xn[:, :, :].rearrange("p t e -> p (t e)")
        rope_a = [xflat[:, (0 + n) * BLK:(1 + n) * BLK] for n in range(2)]
        rope_b = [xflat[:, (2 + n) * BLK:(3 + n) * BLK] for n in range(2)]
        attnT = mix[:, :, :].rearrange("p e n -> p (e n)").rearrange("p (a n) -> p a n", a=KE)
        denT = xflat.rearrange("p (a n) -> p a n", a=KE)

        x_in = [sem(f"x_in{q}") for q in range(NBLK)]
        tables_in, w_qk_in, w_gu_in, w_dn_in = sem("tables_in"), sem("w_qk_in"), sem("w_gu_in"), sem("w_dn_in")
        w_o_in = sem("w_o_in")
        filled = sem("filled")
        vec = sem("vec")
        var_ready, root_ready, xn_ready = sem("var_ready"), sem("root_ready"), sem("xn_ready")
        turned, turned_a, turned_d = sem("turned"), sem("turned_a"), sem("turned_d")
        qk_ready, qk_read, rope_sum = sem("qk_ready"), sem("qk_read"), sem("rope_sum")
        part1, rest1, part2, part3 = sem("part1"), sem("rest1"), sem("part2"), sem("part3")
        stacked = [sem(f"stacked{n}") for n in range(2)]
        vr_ready, vr_read = sem("vr_ready"), sem("vr_read")
        top_max, top_exp = sem("top_max"), sem("top_exp")
        comb_ready, comb_turned, comb_kept, comb_stored = (
            sem("comb_ready"), sem("comb_turned"), sem("comb_kept"), sem("comb_stored"))
        mix_in = [sem(f"mix_in{e}") for e in range(EXP)]
        gu_ready, silu_done, hid_done, hid_mixed, down_done, res_done = (
            sem("gu_ready"), sem("silu_done"), sem("hid_done"), sem("hid_mixed"), sem("down_done"), sem("res_done"))
        qk1_in = [sem(f"qk1_in{n}") for n in range(2)]
        qk2_in = [sem(f"qk2_in{n}") for n in range(2)]
        m_ready, m_done, neg_ready = sem("m_ready"), sem("m_done"), sem("neg_ready")
        s_ready, s_done = sem("s_ready"), sem("s_done")
        rest_done, parts_ready, rows_stored = sem("rest_done"), sem("parts_ready"), sem("rows_stored")
        rows_in = [sem(f"rows_in{n}") for n in range(2)]
        v_ready, pv_done, pv_read = sem("v_ready"), sem("pv_done"), sem("pv_read")
        heads_free = [sem(f"heads_free{n}") for n in range(2)]
        attn_in, den_in = sem("attn_in"), sem("den_in")
        den_done, attn_done, o_ready, o_done, out_sent = (
            sem("den_done"), sem("attn_done"), sem("o_ready"), sem("o_done"), sem("out_sent"))

        RQ = KE * NBLK
        ROPES = RQ + QH

        def rope_order():
            order = []
            for q in range(NBLK):
                order += [("q", a, q) for a in range(KE)]
                if q >= QH:
                    order.append(("k", 0, q - QH))
            return order

        ROPE = rope_order()

        def entries(t):
            return 1 + 2 * t + min((t + LEAD - 1) // STEPS, G - 1)

        def turn_entry(g):
            return 0 if g == 0 else entries(STEPS * g - LEAD) + 2

        def pair_entry(n):
            return entries(n // 2) + n % 2

        def unit_of(u):
            return u // 4 % KT, u // 2 % 2, u // 32 * 2 + u % 2

        def m_bank(m):
            first = AHEAD + UPS * ROT
            last = first + UPS * LSTEPS * TURNS
            if m < first:
                return m % 3
            return (m - first) % (UPS * LSTEPS) % 3 if m < last else (m - last) % 3

        def m_before(m):
            first = AHEAD + UPS * ROT
            last = first + UPS * LSTEPS * TURNS
            at = m if m < first else (m - first) % (UPS * LSTEPS) if m < last else m - last
            return m - 1 if at < 3 and m >= first else m - 2

        def s_slot(e):
            return bank[e % 2]

        def steps(eng, one):
            for t in range(ROT):
                one(t, 0)
            with eng.Fori(0, TURNS) as i:
                for t in range(ROT, ROT + LSTEPS):
                    one(t, i)
            for t in range(ROT + TURNS * LSTEPS, G * STEPS):
                one(t, 0)

        def tiles(eng, one):
            for f in range(FROT):
                one(f, 0)
            with eng.Fori(0, NBLK - 1) as i:
                for f in range(FROT, FROT + FT):
                    one(f, i)
            for f in range(FROT + (NBLK - 1) * FT, NBLK * FT + LAG):
                one(f, 0)

        block = ctx.enter_context(nc.Block())

        @block.sync
        def _(sp):
            xv = x.rearrange("(t p) e -> p t e", p=P)
            for q in range(NBLK):
                sp.dma_start(res[:, q * TB:(q + 1) * TB, :], xv[:, q * TB:(q + 1) * TB, :]).then_inc(x_in[q], 16)
            sp.dma_start(w_gu[:, :, :, :, :], wgu).then_inc(w_gu_in, 16)
            sp.dma_start(w_dn[:, :, :], wdn).then_inc(w_dn_in, 16)
            sp.dma_start(w_o[:, :, :], wo).then_inc(w_o_in, 16)

            for r, (kind, a, q) in enumerate(ROPE):
                sp.wait_ge(part3, r + 1)
                for j in range(NP):
                    if kind == "q":
                        to = q_stacks.rearrange("(b k) r j d s -> b j (k r) d s", b=B)[
                            q // QH, j, a * 16:(a + 1) * 16, :, (q % QH) * BLK:(q % QH + 1) * BLK]
                        part = QPART[j]
                    else:
                        to = k_stacks.rearrange("g j d s -> j g d s")[j, :, :, q * BLK:(q + 1) * BLK]
                        part = KPART[j]
                    sp.dma_start(to, parts[:, r % 2, part, :]).then_inc(stacked[r % 2], 16)

            sp.wait_ge(comb_kept, 1)
            sp.dma_start(weights_by_expert.rearrange("e (t p) -> (e t) p", p=P), combT[:, :]).then_inc(comb_stored, 16)
            sp.wait_ge(comb_stored, 16)

            def load_mix(blk, e):
                sp.dma_start(mix[:, e, :], weights_by_expert[e:e + 1, bass.ds(blk * BLK, BLK)].to_broadcast((P, BLK))
                             ).then_inc(mix_in[e], 16)

            for e in range(EXP):
                load_mix(0, e)
            with sp.Fori(0, NBLK - 1) as i:
                for e in range(EXP):
                    sp.wait_ge(hid_mixed, e + 1 + EXP * i)
                    load_mix(i + 1, e)

            for n in range(2):
                sp.wait_ge(stacked[n], 16 * NP * (ROPES // 2))
            sp.wait_ge(filled, 4)

            def load_stacks(q_to, k_to, g, n, landed):
                for h in range(2):
                    rows = slice(SH * h, SH * h + SR)
                    sp.dma_start(q_to[rows, n, :, :], q_stacks.rearrange("g (a b) j d s -> g b (j d) a s", b=2)[
                        bass.ds(g, 1), h, :, :, :].rearrange("o r a s -> (o r) a s")).then_inc(landed, 16)
                    sp.dma_start(k_to[rows, n, :], k_stacks.rearrange("g j d s -> g (j d) s")[
                        bass.ds(g, 1), :, :].rearrange("o r s -> (o r) s")).then_inc(landed, 16)

            def maxima_rows(g, n, i):
                sp.wait_ge(parts_ready, g + 1 + 2 * i)
                for h in range(REP):
                    sp.dma_start(max_rows[n, h // 2, h % 2].rearrange("m (t p) -> t m p", p=P),
                                 neg_parts[h * KT:(h + 1) * KT, :, :]).then_inc(rows_stored, 16)
                sp.wait_ge(rows_stored, 16 * REP * (g + 1) + 32 * REP * i)
                for h in range(2):
                    sp.dma_start(q2[SH * h + SR:SH * h + SR + MR, n, :, :],
                                 max_rows[n, :, h].rearrange("a m s -> m a s")).then_inc(rows_in[n], 16)

            def send_heads(k, g_dyn, i):
                sp.wait_ge(pv_read, k + 1 + 4 * i)
                for j in range(REP):
                    sp.dma_start(heads_out.rearrange("g r d s -> (g r) d s")[
                        bass.ds(g_dyn * REP + j, 1), :, (k % 2) * BLK:(k % 2 + 1) * BLK].rearrange("o d s -> (o d) s"),
                        heads[32 * j:32 * j + D + 1, k % 2, :]).then_inc(heads_free[k % 2], 16)

            load_stacks(q1, k1, 0, 0, qk1_in[0])
            load_stacks(q1, k1, 1, 1, qk1_in[1])
            load_stacks(q2, k2, 0, 0, qk2_in[0])
            maxima_rows(0, 0, 0)

            def one(t, i):
                g, s = t // STEPS, t % STEPS
                gd = g + 2 * i
                if s == 1 and g >= 1:
                    send_heads(2 * g - 1, gd - 1, i)
                if s == 4:
                    if g + 1 < G:
                        sp.wait_ge(s_ready, entries(g * STEPS) + (2 * LSTEPS + 2) * i)
                        load_stacks(q2, k2, gd + 1, (g + 1) % 2, qk2_in[(g + 1) % 2])
                    if g + 2 < G:
                        sp.wait_ge(m_ready, UNITS * (g + 1) + 2 * UNITS * i)
                        load_stacks(q1, k1, gd + 2, g % 2, qk1_in[g % 2])
                if s == 11:
                    send_heads(2 * g, gd, i)
                if s == 15 and g + 1 < G:
                    maxima_rows(g + 1, (g + 1) % 2, i)

            steps(sp, one)
            send_heads(2 * G - 1, G - 1, 0)

            for n in range(2):
                sp.wait_ge(heads_free[n], 16 * REP * (G + 1))
            for a in range(KE):
                for b in range(B):
                    rows = heads_out.rearrange("(b a k) r d s -> b a (k r) d s", b=B, a=KE)[b, a]
                    sp.dma_start(attnT[:, a, b * S:(b + 1) * S], rows[:, 0:D, :]).then_inc(attn_in, 16)
                    sp.dma_start(denT[:, a, b * S:(b + 1) * S], rows[:, D:D + 1, :].to_broadcast((16, D, S))
                                 ).then_inc(den_in, 16)
            ov = out.rearrange("(t p) e -> p t e", p=P)
            for q in range(NBLK):
                sp.wait_ge(o_done, TB * (q + 1))
                sp.dma_start(ov[:, q * TB:(q + 1) * TB, :], res[:, q * TB:(q + 1) * TB, :]).then_inc(out_sent, 16)
            sp.wait_ge(out_sent, 16 * NBLK)

        @block.gpsimd
        def _(pool):
            for n in range(2):
                pool.sem_inc(heads_free[n], 16 * REP)
            pool.memset(q1[:, :, :, :], 0.0).then_inc(filled, 1)
            pool.memset(q2[:, :, :, :], 0.0).then_inc(filled, 1)
            pool.memset(k1[:, :, :], 1.0).then_inc(filled, 1)
            pool.memset(k2[:, :, :], 1.0).then_inc(filled, 1)
            pool.memset(v_now[:, :, :, :], 1.0).then_inc(filled, 1)
            pool.memset(zeros[:, :], 0.0).then_inc(filled, 1)

            for r in range(ROPES):
                pool.wait_ge(qk_read, 2 * (r + 1))
                pool.tensor_tensor(rope_a[r % 2], rope_a[r % 2], rope_b[r % 2], ALU.add).then_inc(rope_sum, 1)
                pool.wait_ge(part2, r + 1)
                pool.tensor_tensor(parts[:, r % 2, 2, :], rope_b[r % 2], parts[:, r % 2, 1, :], ALU.subtract
                                   ).then_inc(part3, 1)

            def mixed(f, i):
                blk, m = f // FT, f % FT
                if m < 2 or blk >= NBLK:
                    return
                e = m - 2
                pool.wait_ge(hid_done, f + 1 + FT * i)
                pool.wait_ge(mix_in[e], 16 * (blk + 1) + 16 * i)
                pool.tensor_tensor(hid[:, f % HSLOTS, :], hid[:, f % HSLOTS, :], mix[:, e, :], ALU.mult
                                   ).then_inc(hid_mixed, 1)

            tiles(pool, mixed)

            def values(g, n):
                v = v_all[:, :, :, :, :].rearrange("p b k t d -> p (b k) t d")[:, bass.ds(g, 1), :, :].rearrange(
                    "p o t d -> p (o t) d")
                pool.tensor_tensor(v_now[:, n, :, 0:D], v,
                                   zeros[:, 0:KT * D].rearrange("p (t d) -> p t d", t=KT), ALU.add).then_inc(v_ready, 1)

            def split_maxima(g, i):
                ent = turn_entry(g) + 1
                pool.wait_ge(s_done, ent + (2 * LSTEPS + 2) * i)
                if g > 0:
                    pool.wait_ge(rows_stored, 16 * REP * g + 32 * REP * i)
                pool.tensor_tensor(neg_parts[:, 0, :], neg_maxT[:, :], zeros[0:REP * KT, :], ALU.add
                                   ).then_inc(rest_done, 1)
                pool.wait_ge(rest_done, 3 * g + 1 + 6 * i)
                pool.tensor_tensor(neg_parts[:, 1, :], neg_maxT[:, :], neg_parts[:, 0, :], ALU.subtract
                                   ).then_inc(rest_done, 1)
                pool.tensor_tensor(neg_rest[:, :], neg_maxT[:, :], neg_parts[:, 0, :], ALU.subtract
                                   ).then_inc(rest_done, 1)
                pool.wait_ge(rest_done, 3 * g + 3 + 6 * i)
                pool.tensor_tensor(neg_parts[:, 2, :], neg_rest[:, :], neg_parts[:, 1, :], ALU.subtract
                                   ).then_inc(parts_ready, 1)

            pool.wait_ge(vr_read, 2 * NBLK)
            pool.wait_ge(filled, 6)
            values(0, 0)
            split_maxima(0, 0)

            def one(t, i):
                g, s = t // STEPS, t % STEPS
                if s == 3 and g + 1 < G:
                    if g >= 1:
                        pool.wait_ge(pv_done, STEPS // 2 * g + STEPS * i)
                    values(g + 1 + 2 * i, (g + 1) % 2)
                if s == STEPS - LEAD + 1 and g + 1 < G:
                    split_maxima(g + 1, i)

            steps(pool, one)

        @block.scalar
        def _(act):
            act.dma_start(w_qk[:, :, :, :], wqkv).then_inc(w_qk_in, 16)
            act.dma_start(w_vr[:, :, :], wvr).then_inc(w_qk_in, 16)
            act.dma_start(ident[:, :], tables[:, 0:P]).then_inc(tables_in, 16)
            act.dma_start(before[:, :], tables[:, P:P + EXP * EXP]).then_inc(tables_in, 16)
            act.dma_start(cos_sin[:, :, :], tables[:, P + EXP * EXP:].rearrange("p (c s) -> p c s", c=2)
                          ).then_inc(tables_in, 16)
            act.wait_ge(var_ready, 1)
            act.activation(ln[:, 1, :], ln[:, 0, :], ACT.Sqrt).then_inc(root_ready, 1)
            for q in range(NBLK):
                act.wait_ge(turned, 2 * q + 1)
                act.activation(xnT[:, 0, q * BLK:(q + 1) * BLK], pb(2 * q), ACT.Copy).then_inc(turned_a, 1)

            vq = 0
            for r, (kind, a, q) in enumerate(ROPE):
                act.wait_ge(rope_sum, r + 1)
                if r >= 2:
                    act.wait_ge(stacked[r % 2], 16 * NP * (r // 2))
                act.activation(parts[:, r % 2, 0, :], rope_a[r % 2], ACT.Copy).then_inc(part1, 1)
                act.wait_ge(rest1, r + 1)
                act.activation(parts[:, r % 2, 1, :], rope_b[r % 2], ACT.Copy).then_inc(part2, 1)
                if kind == "q" and a == 1:
                    act.wait_ge(vr_ready, vq + 1)
                    vr = pb(6 + vq % 2)[:, 0:TB * (KV * D + EXP)].rearrange("p (t c) -> p t c", t=TB)
                    b, t0 = vq // QH, (vq % QH) * TB
                    act.activation(v_all[:, b, :, t0:t0 + TB, :].rearrange("p k t d -> p t k d"),
                                   vr[:, :, 0:KV * D].rearrange("p t (k d) -> p t k d", k=KV), ACT.Copy
                                   ).then_inc(vr_read, 1)
                    act.activation(logits[:, vq * TB:(vq + 1) * TB, :], vr[:, :, KV * D:], ACT.Copy
                                   ).then_inc(vr_read, 1)
                    vq += 1
            act.wait_ge(top_max, 1)
            act.activation(rt[:, 1, :, :], rt[:, 0, :, :], ACT.Exp).then_inc(top_exp, 1)

            def gated(f, i):
                if f >= NBLK * FT:
                    return
                if f == 2:
                    act.wait_ge(comb_turned, 1)
                    act.activation(combT[:, :], pb(7)[:, 0:P], ACT.Copy).then_inc(comb_kept, 1)
                act.wait_ge(gu_ready, f + 1 + FT * i)
                if f >= HSLOTS:
                    act.wait_ge(down_done, f - HSLOTS + 1 + FT * i)
                act.activation(hid[:, f % HSLOTS, :], pb(2 * (f % 2)), ACT.Silu).then_inc(silu_done, 1)

            tiles(act, gated)

            def turned_maxima(g, i):
                ent = turn_entry(g)
                act.wait_ge(s_ready, ent + 1 + (2 * LSTEPS + 2) * i)
                if g > 0:
                    act.wait_ge(parts_ready, g + 2 * i)
                act.activation(neg_maxT[:, :], s_slot(ent)[0:REP * KT, 0:P], ACT.Copy).then_inc(s_done, 1)

            turned_maxima(0, 0)

            def keep_heads(k, i):
                act.wait_ge(pv_done, KT // 2 * (k + 1) + STEPS * i)
                act.wait_ge(heads_free[k % 2], 16 * REP * (k // 2 + 1) + 32 * REP * i)
                act.activation(heads[:, k % 2, :], pb(7), ACT.Copy).then_inc(pv_read, 1)

            def one(t, i):
                g, s = t // STEPS, t % STEPS
                for n in (2 * t, 2 * t + 1):
                    act.wait_ge(s_ready, pair_entry(n) + 1 + (2 * LSTEPS + 2) * i)
                    if n % 4 == 0 and n >= PSLOTS:
                        act.wait_ge(pv_done, n // 4 - 1 + STEPS * i)
                    act.activation(probs[:, n % PSLOTS, :], s_slot(pair_entry(n))[:, :], ACT.Exp, scale=SCALE
                                   ).then_inc(s_done, 1)
                if s == STEPS - LEAD and g + 1 < G:
                    turned_maxima(g + 1, i)
                if t >= KT and t % KT == 0:
                    keep_heads(t // KT - 1, i)

            steps(act, one)
            keep_heads(2 * G - 1, 0)

        @block.vector
        def _(dve):
            chain = [0]

            def link(ins):
                chain[0] += 1
                ins.then_inc(vec, 1)
                dve.wait_ge(vec, chain[0])

            for q in range(NBLK):
                dve.wait_ge(x_in[q], 16)
                for t in range(q * TB, (q + 1) * TB):
                    last = nc.vector.bn_stats(stats[:, t, :], res[:, t, :])
            link(last)
            for t in range(NT):
                last = nc.vector.bn_aggr(mv[:, t, :], stats[:, t, :])
            link(last)
            nc.vector.tensor_scalar(ln[:, 0, :], mv[:, :, 1], EPS, None, ALU.add).then_inc(var_ready, 1)
            dve.wait_ge(root_ready, 1)
            link(nc.vector.reciprocal(ln[:, 2, :], ln[:, 1, :]))
            link(nc.vector.tensor_tensor(ln[:, 3, :], ln[:, 2, :], ln[:, 2, :], ALU.mult))
            link(nc.vector.tensor_tensor(ln[:, 1, :], ln[:, 3, :], ln[:, 0, :], ALU.mult))
            link(nc.vector.tensor_scalar(ln[:, 3, :], ln[:, 1, :], -0.5, 1.5, ALU.mult, ALU.add))
            link(nc.vector.tensor_tensor(ln[:, 1, :], ln[:, 2, :], ln[:, 3, :], ALU.mult))
            for t in range(NT):
                nc.vector.tensor_scalar(xn[:, t, :], res[:, t, :], mv[:, t, 0:1], ln[:, 1, t:t + 1],
                                        ALU.subtract, ALU.mult).then_inc(xn_ready, 1)
            for q in range(NBLK):
                dve.wait_ge(turned, 2 * q + 2)
                nc.vector.tensor_copy(xnT[:, 1, q * BLK:(q + 1) * BLK], pb(2 * q + 1)).then_inc(turned_d, 1)

            dve.wait_ge(tables_in, 48)
            for r, (kind, a, q) in enumerate(ROPE):
                pos = slice((q % QH) * BLK, (q % QH + 1) * BLK)
                dve.wait_ge(qk_ready, r + 1)
                if r >= 2:
                    dve.wait_ge(part3, r - 1)
                nc.vector.tensor_tensor(rope_a[r % 2], pb(2 * (r % 3)), cos_sin[:, 0, pos], ALU.mult
                                        ).then_inc(qk_read, 1)
                nc.vector.tensor_tensor(rope_b[r % 2], pb(2 * (r % 3) + 1), cos_sin[:, 1, pos], ALU.mult
                                        ).then_inc(qk_read, 1)
                dve.wait_ge(part1, r + 1)
                nc.vector.tensor_tensor(rope_b[r % 2], rope_a[r % 2], parts[:, r % 2, 0, :], ALU.subtract
                                        ).then_inc(rest1, 1)

            dve.wait_ge(vr_read, 2 * NBLK)
            link(nc.vector.tensor_reduce(rs[:, 0, :], logits[:, :, :], AX.X, ALU.max))
            nc.vector.tensor_tensor(rt[:, 0, :, :], logits[:, :, :],
                                    rs[:, 0, :].unsqueeze(2).to_broadcast((P, NT, EXP)), ALU.subtract
                                    ).then_inc(top_max, 1)
            dve.wait_ge(top_exp, 1)
            link(nc.vector.tensor_reduce(rs[:, 0, :], rt[:, 1, :, :], AX.X, ALU.add))
            link(nc.vector.reciprocal(rs[:, 1, :], rs[:, 0, :]))
            link(nc.vector.tensor_tensor(rt[:, 0, :, :], rt[:, 1, :, :],
                                         rs[:, 1, :].unsqueeze(2).to_broadcast((P, NT, EXP)), ALU.mult))
            pj = rt[:, 0, :, :].unsqueeze(2).to_broadcast((P, NT, EXP, EXP))
            pe_ = rt[:, 0, :, :].unsqueeze(3).to_broadcast((P, NT, EXP, EXP))
            nc.vector.tensor_tensor(rank[:, 0], pj, pe_, ALU.is_gt)
            link(nc.vector.tensor_tensor(rank[:, 1], pj, pe_, ALU.is_equal))
            link(nc.vector.tensor_tensor(
                rank[:, 1], rank[:, 1],
                before[:, :].rearrange("p (o e j) -> p o e j", o=1, e=EXP).to_broadcast((P, NT, EXP, EXP)), ALU.mult))
            link(nc.vector.tensor_tensor(rank[:, 0], rank[:, 0], rank[:, 1], ALU.add))
            link(nc.vector.tensor_reduce(rt[:, 1, :, :], rank[:, 0], AX.X, ALU.add))
            nc.vector.scalar_tensor_tensor(comb[:, :, :].rearrange("p e t -> p t e"), rt[:, 1, :, :], 2.0,
                                           rt[:, 0, :, :], ALU.is_lt, ALU.mult).then_inc(comb_ready, 1)

            def tile(f, i):
                if f < NBLK * FT:
                    dve.wait_ge(silu_done, f + 1 + FT * i)
                    nc.vector.tensor_tensor(hid[:, f % HSLOTS, :], hid[:, f % HSLOTS, :], pb(2 * (f % 2) + 1),
                                            ALU.mult).then_inc(hid_done, 1)
                if f >= FT and (f - LAG) % FT == FT - 1:
                    blk = (f - LAG) // FT
                    dve.wait_ge(down_done, FT * (blk + 1) + FT * i)
                    for t in range(TB):
                        at = bass.ds((blk + i) * TB + t, 1)
                        r = res[:, at, :].rearrange("p o e -> p (o e)")
                        nc.vector.tensor_tensor(r, pb(4 + t)[:, 0:E], r, ALU.add).then_inc(res_done, 1)

            tiles(dve, tile)

            def unit(m, i):
                g, u = m // UNITS, m % UNITS
                qt, kh, h = unit_of(u)
                if u == 0 and g >= 2:
                    dve.wait_ge(neg_ready, g - 1 + 2 * i)
                dve.wait_ge(m_ready, m + 1 + 2 * UNITS * i)
                col = (h * KT + qt) * 2 + kh
                nc.vector.tensor_reduce(unit_max[:, g % 2, col:col + 1], pb(4 + m_bank(m)), AX.X, ALU.max
                                        ).then_inc(m_done, 1)
                if u == UNITS - 1:
                    dve.wait_ge(m_done, m + 1 + 2 * UNITS * i)
                    if g >= 1:
                        dve.wait_ge(s_ready, turn_entry(g - 1) + 1 + (2 * LSTEPS + 2) * i)
                    nc.vector.tensor_reduce(neg_max[:, g % 2, :],
                                            unit_max[:, g % 2, :].rearrange("p (c k) -> p c k", k=2), AX.X, ALU.max,
                                            negate=True).then_inc(neg_ready, 1)

            for m in range(AHEAD):
                unit(m, 0)

            def one(t, i):
                for m in range(AHEAD + UPS * t, AHEAD + UPS * (t + 1)):
                    if m < G * UNITS:
                        unit(m, i)

            steps(dve, one)

            for a in range(KE):
                if a == 0:
                    dve.wait_ge(den_in, 16 * KE * B)
                    dve.wait_ge(attn_in, 16 * KE * B)
                nc.vector.reciprocal(denT[:, a, :], denT[:, a, :]).then_inc(den_done, 1)
                dve.wait_ge(den_done, a + 1)
                nc.vector.tensor_tensor(attnT[:, a, :], attnT[:, a, :], denT[:, a, :], ALU.mult).then_inc(attn_done, 1)
            for t in range(NT):
                dve.wait_ge(o_ready, t + 1)
                nc.vector.tensor_tensor(res[:, t, :], pb(t % 8)[:, 0:E], res[:, t, :], ALU.add).then_inc(o_done, 1)

        @block.tensor
        def _(pe):
            pe.wait_ge(tables_in, 48)
            for q in range(NBLK):
                pe.wait_ge(xn_ready, TB * (q + 1))
                for k in range(KE):
                    for t in range(TB):
                        last = nc.tensor.transpose(pb(2 * q + k)[:, t * P:(t + 1) * P],
                                                   xn[:, q * TB + t, k * P:(k + 1) * P], ident[:, :])
                    last.then_inc(turned, 1)

            pe.wait_ge(w_qk_in, 32)
            pe.wait_ge(turned_a, NBLK)
            pe.wait_ge(turned_d, NBLK)
            vq = 0
            for r, (kind, a, q) in enumerate(ROPE):
                if r >= 3:
                    pe.wait_ge(qk_read, 2 * (r - 2))
                for rot in range(2):
                    to = pb(2 * (r % 3) + rot)
                    if kind == "q":
                        for k in range(KE):
                            last = nc.tensor.matmul(to, w_qk[:, k, rot, a * P:(a + 1) * P],
                                                    xnT[:, k, q * BLK:(q + 1) * BLK], start=(k == 0), stop=(k == KE - 1))
                    else:
                        for k in range(KE):
                            for b in range(B):
                                tok = b * S + q * BLK
                                last = nc.tensor.matmul(to[b * SH:(b + 1) * SH, :], w_qk[:, k, rot, 2 * P:2 * P + SH],
                                                        xnT[:, k, tok:tok + BLK], start=(k == 0), stop=(k == KE - 1))
                last.then_inc(qk_ready, 1)
                if kind == "q" and a == 1:
                    if vq >= 2:
                        pe.wait_ge(vr_read, 2 * (vq - 1))
                    for t in range(TB):
                        C = KV * D + EXP
                        for k in range(KE):
                            last = nc.tensor.matmul(pb(6 + vq % 2)[:, t * C:(t + 1) * C],
                                                    xnT[:, k, vq * BLK + t * P:vq * BLK + (t + 1) * P],
                                                    w_vr[:, k, :], start=(k == 0), stop=(k == KE - 1))
                    last.then_inc(vr_ready, 1)
                    vq += 1

            pe.wait_ge(w_gu_in, 16)
            pe.wait_ge(w_dn_in, 16)
            pe.wait_ge(qk_read, 2 * ROPES)
            pe.wait_ge(vr_read, 2 * NBLK)

            def tile(f, i):
                if f < NBLK * FT:
                    blk, m = f // FT, f % FT
                    if f >= 2:
                        pe.wait_ge(hid_done, f - 1 + FT * i)
                    for w in range(2):
                        for k in range(KE):
                            last = nc.tensor.matmul(pb(2 * (f % 2) + w), w_gu[:, k, m, w, :],
                                                    xnT[:, k, bass.ds((blk + i) * BLK, BLK)],
                                                    start=(k == 0), stop=(k == KE - 1))
                    last.then_inc(gu_ready, 1)
                if f == 1:
                    pe.wait_ge(comb_ready, 1)
                    nc.tensor.transpose(pb(7)[:, 0:P], comb[:, :, :].rearrange("p e t -> p (e t)"), ident[:, :]
                                        ).then_inc(comb_turned, 1)
                if f >= LAG:
                    d = f - LAG
                    blk, m = d // FT, d % FT
                    if m < 2:
                        pe.wait_ge(hid_done, d + 1 + FT * i)
                    else:
                        pe.wait_ge(hid_mixed, EXP * blk + m - 1 + EXP * i)
                    if m == 0:
                        if blk == 0:
                            pe.wait_ge(comb_kept, 1)
                        else:
                            pe.wait_ge(res_done, TB * blk + TB * i)
                    for t in range(TB):
                        last = nc.tensor.matmul(pb(4 + t)[:, 0:E], hid[:, d % HSLOTS, t * P:(t + 1) * P],
                                                w_dn[:, m, :], start=(m == 0), stop=(m == FT - 1))
                    last.then_inc(down_done, 1)

            tiles(pe, tile)

            pe.wait_ge(res_done, NT)
            pe.wait_ge(hid_done, NBLK * FT)

            def unit(m, i):
                g, u = m // UNITS, m % UNITS
                qt, kh, h = unit_of(u)
                n = g % 2
                if u == 0:
                    pe.wait_ge(qk1_in[n], 64 * (g // 2 + 1) + 64 * i)
                if m >= 3:
                    pe.wait_ge(m_done, m_before(m) + 2 * UNITS * i)
                rows = slice(SH * (h % 2), SH * (h % 2) + SH)
                nc.tensor.matmul(pb(4 + m_bank(m)), q1[rows, n, h // 2, qt * P:(qt + 1) * P],
                                 k1[rows, n, kh * BLK:(kh + 1) * BLK], start=True, stop=True).then_inc(m_ready, 1)

            def turn_maxima(g, i):
                ent = turn_entry(g)
                pe.wait_ge(neg_ready, g + 1 + 2 * i)
                if ent >= 2:
                    pe.wait_ge(s_done, ent - 1 + (2 * LSTEPS + 2) * i)
                nc.tensor.transpose(s_slot(ent)[0:REP * KT, 0:P], neg_max[:, g % 2, :], ident[:, :]).then_inc(s_ready, 1)

            def scores(n, i):
                g, s = n // 2 // STEPS, n // 2 % STEPS
                qh, kt = s // KT, s % KT
                e = pair_entry(n)
                if e >= 2:
                    pe.wait_ge(s_done, e - 1 + (2 * LSTEPS + 2) * i)
                for h in range(2):
                    rows = slice(SH * h, SH * h + SH)
                    last = nc.tensor.matmul(s_slot(e)[:, h * BLK:(h + 1) * BLK], k2[rows, g % 2, kt * P:(kt + 1) * P],
                                            q2[rows, g % 2, n % 2, qh * BLK:(qh + 1) * BLK], start=True, stop=True)
                last.then_inc(s_ready, 1)

            def weigh_values(b, i):
                g = b // (STEPS // 2)
                k = b // (KT // 2)
                if b % (KT // 2) == 0 and k >= 1:
                    pe.wait_ge(pv_read, k + 4 * i)
                pe.wait_ge(s_done, pair_entry(4 * b + 3) + 1 + (2 * LSTEPS + 2) * i)
                for s in (2 * b, 2 * b + 1):
                    kt = s % KT
                    for h in range(REP):
                        n = 2 * s + h // 2
                        last = nc.tensor.matmul(pb(7)[32 * h:32 * h + 32, :], v_now[:, g % 2, kt, :],
                                                probs[:, n % PSLOTS, (h % 2) * BLK:(h % 2 + 1) * BLK],
                                                start=(kt == 0), stop=(kt == KT - 1))
                last.then_inc(pv_done, 1)

            for m in range(AHEAD):
                unit(m, 0)
            turn_maxima(0, 0)

            def one(t, i):
                g, s = t // STEPS, t % STEPS
                if s == 0:
                    pe.wait_ge(qk2_in[g % 2], 64 * (g // 2 + 1) + 64 * i)
                    pe.wait_ge(rows_in[g % 2], 32 * (g // 2 + 1) + 32 * i)
                for n in range(2):
                    scores(2 * t + n, i)
                    for m in range(AHEAD + UPS * t + 2 * n, AHEAD + UPS * t + 2 * n + 2):
                        if m < G * UNITS:
                            unit(m, i)
                if s == STEPS - LEAD and g + 1 < G:
                    turn_maxima(g + 1, i)
                if t >= 2 and t % 2 == 0:
                    if s == 2:
                        pe.wait_ge(v_ready, g + 1 + 2 * i)
                    weigh_values(t // 2 - 1, i)

            steps(pe, one)
            weigh_values(G * STEPS // 2 - 1, 0)

            pe.wait_ge(attn_done, KE)
            pe.wait_ge(w_o_in, 16)
            for t in range(NT):
                if t == 0:
                    pe.wait_ge(pv_read, 2 * G)
                    pe.wait_ge(m_done, G * UNITS)
                if t >= 8:
                    pe.wait_ge(o_done, t - 7)
                for a in range(KE):
                    last = nc.tensor.matmul(pb(t % 8)[:, 0:E], attnT[:, a, t * P:(t + 1) * P], w_o[:, a, :],
                                            start=(a == 0), stop=(a == KE - 1))
                last.then_inc(o_ready, 1)


def kernel(L0_attn_x, L0_attn_Wq, L0_attn_Wk, L0_attn_Wv, L0_attn_Wo, L0_ffn_router_w, L0_ffn_shared_gate,
           L0_ffn_shared_up, L0_ffn_shared_down, L0_ffn_w_gate, L0_ffn_w_up, L0_ffn_w_down):
    import concourse.bacc as bacc
    from concourse.bass_utils import run_bass_kernel_spmd

    def a(v):
        return np.asarray(v)

    swap = np.arange(E).reshape(-1, 2, HALF)[:, ::-1].reshape(-1)
    wq, wk, wv = a(L0_attn_Wq), a(L0_attn_Wk), a(L0_attn_Wv)
    plain = np.concatenate([wq, wk])
    other = np.concatenate([wq[swap], wk[swap[:KV * D]]])
    wqkv = np.stack([plain.T, other.T], 1).reshape(KE, P, 2, -1).transpose(1, 0, 2, 3)
    wvr = np.concatenate([wv.T, a(L0_ffn_router_w)], 1).reshape(KE, P, -1).transpose(1, 0, 2)
    wo = a(L0_attn_Wo).T.reshape(KE, P, E).transpose(1, 0, 2)
    sg, su, eg, eu = a(L0_ffn_shared_gate), a(L0_ffn_shared_up), a(L0_ffn_w_gate), a(L0_ffn_w_up)
    gate = np.concatenate([sg, eg.transpose(1, 0, 2).reshape(E, -1)], 1).reshape(E, FT, P)
    up = np.concatenate([su, eu.transpose(1, 0, 2).reshape(E, -1)], 1).reshape(E, FT, P)
    wgu = np.stack([gate, up], 2).reshape(KE, P, FT, 2, P).transpose(1, 0, 2, 3, 4)
    wdn = np.concatenate([a(L0_ffn_shared_down).reshape(2, P, E), a(L0_ffn_w_down)]).transpose(1, 0, 2)

    f = np.float32
    inv = (f(1.0) / np.power(f(10000.0), np.arange(0, D, 2, dtype=f) / f(D))).astype(f)
    angle = np.outer(np.arange(S, dtype=f), inv).astype(f)
    cos = np.cos(angle).T[np.arange(P) % HALF]
    sin = np.sin(angle).T[np.arange(P) % HALF]
    sign = np.where(np.arange(P) % D < HALF, f(-1), f(1))[:, None]
    before = np.broadcast_to(np.tril(np.ones((EXP, EXP), f), -1).reshape(1, -1), (P, EXP * EXP))
    tables = np.concatenate([np.eye(P, dtype=f), before, cos, sin * sign], 1).astype(f)

    arrays = {"x": a(L0_attn_x).reshape(N, E), "wqkv": wqkv, "wo": wo, "wgu": wgu, "wdn": wdn, "wvr": wvr,
              "tables": tables}
    arrays = {k: np.ascontiguousarray(v) for k, v in arrays.items()}
    nc = bacc.Bacc("TRN2", target_bir_lowering=False, num_devices=1)
    aps = {k: nc.dram_tensor(k, v.shape, mybir.dt.from_np(v.dtype), kind="ExternalInput").ap()
           for k, v in arrays.items()}
    out = nc.dram_tensor("out", (N, E), F32, kind="ExternalOutput").ap()
    ffn_attention_block(nc, out=out, **aps)
    r = run_bass_kernel_spmd(nc, [arrays], core_ids=[0])
    return r.results[0]["out"].reshape(B, S, E)
```

```python
from contextlib import ExitStack

import numpy as np

import concourse.bass as bass
from concourse import mybir

ALU = mybir.AluOpType
ACT = mybir.ActivationFunctionType
AX = mybir.AxisListType
F32 = mybir.dt.float32
BF16 = mybir.dt.bfloat16

P = 128
B, S, E = 2, 1024, 256
H, KV = 32, 8
D = E // H
REP = H // KV
N = B * S
KE = E // P
BLK = 512
NBLK = N // BLK
TB = BLK // P
NT = N // P
EXP = 8
FT = 2 + EXP
EPS = 1e-5
HALF = D // 2

QPART = (0, 0, 0, 1, 2, 1)
KPART = (2, 1, 0, 0, 0, 1)
NP = len(QPART)
SR = NP * D
MR = 3
SH = 64

G = B * KV
KT = S // P
QH = S // BLK
STEPS = QH * KT
UNITS = REP * (S // P) * (S // BLK)
UPS = UNITS // STEPS
LEAD = 4
AHEAD = UNITS + LEAD * UPS
ROT = 4
LSTEPS = 2 * STEPS
TURNS = (G * STEPS - ROT) // LSTEPS
PSLOTS = 4
VW = 32
SCALE = 1.0 / float(np.sqrt(D))
FBLK = N // (TURNS + 1)
FTB = FBLK // P
SLOTS = 2 * LSTEPS
UP_MM = 2 * KE
DOWN_AT = SLOTS - FT * FTB
GU = 3

def ffn_attention_block(nc, x, wqkv, wo, wgu, wdn, wvr, tables, out):
    ctx = ExitStack()
    with ctx:
        def sb(name, shape, dt=F32):
            return ctx.enter_context(nc.sbuf_tensor(name, shape, dt))

        def sem(name):
            return ctx.enter_context(nc.semaphore(name))

        bank = [ctx.enter_context(nc.psum_tensor(f"bank{n}", [P, 2 * BLK], F32)) for n in range(4)]

        def pb(n):
            return bank[n // 2][:, (n % 2) * BLK:(n % 2 + 1) * BLK]

        q_stacks = nc.dram_tensor("q_stacks", (NP, G * REP * D, S), BF16).ap()
        k_stacks = nc.dram_tensor("k_stacks", (NP, G * D, S), BF16).ap()
        weights_by_expert = nc.dram_tensor("weights_by_expert", (EXP, N), F32).ap()
        max_rows = nc.dram_tensor("max_rows", (2, 2, 2, MR, S), BF16).ap()
        heads_out = nc.dram_tensor("heads_out", (G, REP, D + 1, S), F32).ap()

        res = sb("res", [P, NT, E])
        xn = sb("xn", [P, NT, E])
        xnT = sb("xnT", [P, KE, N])
        w_gu = sb("w_gu", [P, KE, FT, 2, P])
        w_dn = sb("w_dn", [P, FT, E])
        w_o = sb("w_o", [P, KE, E])
        w_qk = sb("w_qk", [P, KE, 2, 2 * P + SH])
        w_vr = sb("w_vr", [P, KE, KV * D + EXP])
        cos_sin = sb("cos_sin", [P, 2, S])
        cos_sin_k = sb("cos_sin_k", [P, 2, BLK])
        ident = sb("ident", [P, P])
        zeros = sb("zeros", [P, P])
        before = sb("before", [P, EXP * EXP])
        mix = sb("mix", [P, EXP, FBLK])
        work = sb("work", [P, FT * FBLK + GU * 3 * FBLK])
        parts = sb("parts", [P, 2, 3, BLK], BF16)
        q1 = sb("q1", [P, 2, 2, S], BF16)
        k1 = sb("k1", [P, 2, S], BF16)
        q2 = sb("q2", [P, 2, 2, S], BF16)
        k2 = sb("k2", [P, 2, S], BF16)
        probs = sb("probs", [P, PSLOTS, 2 * BLK])
        heads = sb("heads", [P, 2, BLK])
        v_all = sb("v_all", [P, B, KV, KT, D])
        v_now = sb("v_now", [P, 2, KT, VW])
        stats = sb("stats", [P, NT, 6])
        mv = sb("mv", [P, NT, 2])
        ln = sb("ln", [P, 4, NT])
        logits = sb("logits", [P, NT, EXP])
        rt = sb("rt", [P, 2, NT, EXP])
        rs = sb("rs", [P, 2, NT])
        comb = sb("comb", [P, EXP, NT])
        combT = sb("combT", [P, P])
        unit_max = sb("unit_max", [P, 2, UNITS])
        neg_max = sb("neg_max", [P, 2, UNITS // 2])
        neg_maxT = sb("neg_maxT", [REP * KT, P])
        neg_rest = sb("neg_rest", [REP * KT, P])
        neg_parts = sb("neg_parts", [REP * KT, MR, P], BF16)
        hid = work[:, 0:FT * FBLK].rearrange("p (m n) -> p m n", m=FT)
        gu = work[:, FT * FBLK:].rearrange("p (o w n) -> p o w n", o=GU, w=3)
        attnT = work[:, 0:KE * N].rearrange("p (a n) -> p a n", a=KE)
        xflat = xn[:, :, :].rearrange("p t e -> p (t e)")
        denT = xflat.rearrange("p (a n) -> p a n", a=KE)
        rank = xflat[:, 0:2 * NT * EXP * EXP].rearrange("p (w t e j) -> p w t e j", w=2, t=NT, e=EXP)
        rope_a = [probs[:, n, 0:BLK] for n in range(2)]
        rope_b = [probs[:, n, BLK:2 * BLK] for n in range(2)]

        x_in = [sem(f"x_in{q}") for q in range(NBLK)]
        tables_in, w_qk_in, w_gu_in, w_dn_in = sem("tables_in"), sem("w_qk_in"), sem("w_gu_in"), sem("w_dn_in")
        w_o_in = sem("w_o_in")
        filled = sem("filled")
        vec = sem("vec")
        var_ready, root_ready, xn_ready = sem("var_ready"), sem("root_ready"), sem("xn_ready")
        turned, turned_a, turned_d = sem("turned"), sem("turned_a"), sem("turned_d")
        qk_ready, qk_read, rope_sum = sem("qk_ready"), sem("qk_read"), sem("rope_sum")
        part1, rest1, part2, part3 = sem("part1"), sem("rest1"), sem("part2"), sem("part3")
        stacked = [sem(f"stacked{n}") for n in range(2)]
        vr_ready, vr_read = sem("vr_ready"), sem("vr_read")
        top_max, top_exp = sem("top_max"), sem("top_exp")
        comb_ready, comb_turned, comb_kept, comb_stored = (
            sem("comb_ready"), sem("comb_turned"), sem("comb_kept"), sem("comb_stored"))
        mix_in = sem("mix_in")
        gu_ready, gu_kept, gu_read, hid_steps, down_done, res_done = (
            sem("gu_ready"), sem("gu_kept"), sem("gu_read"), sem("hid_steps"), sem("down_done"), sem("res_done"))
        qk1_in = [sem(f"qk1_in{n}") for n in range(2)]
        qk2_in = [sem(f"qk2_in{n}") for n in range(2)]
        m_ready, m_done, neg_ready = sem("m_ready"), sem("m_done"), sem("neg_ready")
        s_ready, s_done = sem("s_ready"), sem("s_done")
        rest_done, parts_ready, rows_stored = sem("rest_done"), sem("parts_ready"), sem("rows_stored")
        rows_in = [sem(f"rows_in{n}") for n in range(2)]
        v_ready, pv_done, pv_read = sem("v_ready"), sem("pv_done"), sem("pv_read")
        heads_free = [sem(f"heads_free{n}") for n in range(2)]
        attn_in = [sem(f"attn_in{c}") for c in range(5)]
        den_done, attn_done, o_ready, o_done, out_sent = (
            sem("den_done"), sem("attn_done"), sem("o_ready"), sem("o_done"), sem("out_sent"))

        ROPE = []
        for b in range(B):
            ROPE += [("q", a, QH * b + q) for q in range(QH) for a in range(KE)] + [("k", b, None)]
        ROPES = len(ROPE)

        def stored(r):
            return sum(16 * 3 * (1 if ROPE[j][0] == "q" else 2) for j in range(r % 2, r + 1, 2))

        def hid_count(m):
            return 3 * m + max(m - 2, 0)

        HID = hid_count(FT)

        AHEAD_ORDER = [
            ("norm", 0), ("turn", 0), ("norm", 1), ("rope", 0), ("turn", 1), ("rope", 1), ("vr", 0), ("rest", 0),
            ("norm", 2), ("rope", 2), ("rest", 1), ("rope", 3), ("turn", 2), ("rest", 2), ("vr", 1), ("rope", 4),
            ("rest", 3), ("norm", 3), ("rest", 4), ("loads", 0), ("turn", 3), ("vr", 2), ("vr", 3), ("rope", 5),
            ("rope", 6), ("rest", 5), ("router", 0), ("rest", 6)]
        more = [("rope", 7), ("rope", 8), ("rest", 7), ("rope", 9), ("rest", 8), ("rest", 9), ("comb", 0)]
        slot = 0
        for p in range(AHEAD // 2):
            AHEAD_ORDER += [("m", 2 * p), ("m", 2 * p + 1)]
            if more:
                AHEAD_ORDER.append(more.pop(0))
            elif slot < SLOTS:
                AHEAD_ORDER += [("f", slot), ("f", slot + 1)]
                slot += 2
        AHEAD_ORDER += [("f", j) for j in range(slot, SLOTS)]

        def entries(t):
            return 1 + 2 * t + min((t + LEAD - 1) // STEPS, G - 1)

        def turn_entry(g):
            return 0 if g == 0 else entries(STEPS * g - LEAD) + 2

        def pair_entry(n):
            return entries(n // 2) + n % 2

        def unit_of(u):
            return u // 4 % KT, u // 2 % 2, u // 32 * 2 + u % 2

        def m_bank(m):
            return 4 + m % 2

        PIECES = [(0, KV, None), (KV, KV + 4, None), (KV + 4, G - 1, None), (G - 1, G, 0), (G - 1, G, 1)]
        PIECE_STEPS = [G * STEPS - 20, G * STEPS - 19, G * STEPS - 12, G * STEPS - 4]

        def piece_place(g0, g1, half):
            b, k = g0 // KV, g0 % KV
            rows = slice(k % 4 * REP * D, (k % 4 + g1 - g0) * REP * D)
            return k // 4, b, rows, slice(0, S) if half is None else slice(half * BLK, (half + 1) * BLK)

        def s_slot(e):
            return bank[e % 2]

        def steps(eng, one):
            for t in range(ROT):
                one(t, 0)
            with eng.Fori(0, TURNS) as i:
                for t in range(ROT, ROT + LSTEPS):
                    one(t, i)
            for t in range(ROT + TURNS * LSTEPS, G * STEPS):
                one(t, 0)

        def place(t):
            return (t - ROT) % LSTEPS if ROT <= t < ROT + TURNS * LSTEPS else None

        def ahead(**does):
            for what, n in AHEAD_ORDER:
                if what in does:
                    does[what](n)

        block = ctx.enter_context(nc.Block())

        @block.sync
        def _(sp):
            xv = x.rearrange("(t p) e -> p t e", p=P)
            for q in range(NBLK):
                sp.dma_start(res[:, q * TB:(q + 1) * TB, :], xv[:, q * TB:(q + 1) * TB, :]).then_inc(x_in[q], 16)
            sp.dma_start(w_gu[:, :, :, :, :], wgu).then_inc(w_gu_in, 16)
            sp.dma_start(w_dn[:, :, :], wdn).then_inc(w_dn_in, 16)
            sp.dma_start(w_o[:, :, :], wo).then_inc(w_o_in, 16)

            def store_parts(r):
                kind, a, q = ROPE[r]
                sp.wait_ge(part3, r + 1)
                for part in range(3):
                    js = [j for j in range(NP) if (QPART if kind == "q" else KPART)[j] == part]
                    js = slice(js[0], js[-1] + 1, js[1] - js[0] if len(js) > 1 else 1)
                    for half in range(1 if kind == "q" else 2):
                        if kind == "q":
                            f0 = q // QH * E + a * P
                            to = q_stacks[js, f0:f0 + P, (q % QH) * BLK:(q % QH + 1) * BLK]
                            src = parts[:, r % 2, part, :]
                        else:
                            f0 = a * KV * D
                            to = k_stacks[js, f0:f0 + KV * D, half * BLK:(half + 1) * BLK]
                            src = parts[half * SH:(half + 1) * SH, r % 2, part, :]
                        n, rows = to.shape[0], to.shape[1]
                        sp.dma_start(to.rearrange("j f s -> f j s"), src.unsqueeze(1).to_broadcast((rows, n, BLK))
                                     ).then_inc(stacked[r % 2], 16)

            def load_mix(blk):
                sp.dma_start(mix[:, :, :], weights_by_expert[:, bass.ds(blk * FBLK, FBLK)].unsqueeze(0).to_broadcast(
                    (P, EXP, FBLK))).then_inc(mix_in, 16)

            def comb_out(_):
                sp.wait_ge(comb_kept, 1)
                sp.dma_start(weights_by_expert.rearrange("e (t p) -> (e t) p", p=P), combT[:, :]
                             ).then_inc(comb_stored, 16)
                sp.wait_ge(comb_stored, 16)
                load_mix(0)

            def load_stacks(q_to, k_to, g, n, landed):
                for h in range(REP):
                    at = SH * (h % 2)
                    sp.dma_start(q_to[at:at + SR, n, h // 2, :], q_stacks[:, bass.ds(g * REP * D + h * D, D), :]
                                 ).then_inc(landed, 16)
                for h in range(2):
                    sp.dma_start(k_to[SH * h:SH * h + SR, n, :], k_stacks[:, bass.ds(g * D, D), :]
                                 ).then_inc(landed, 16)

            def maxima_rows(g, n, i):
                sp.wait_ge(parts_ready, g + 1 + 2 * i)
                for h in range(REP):
                    sp.dma_start(max_rows[n, h // 2, h % 2].rearrange("m (t p) -> t m p", p=P),
                                 neg_parts[h * KT:(h + 1) * KT, :, :]).then_inc(rows_stored, 16)
                sp.wait_ge(rows_stored, 16 * REP * (g + 1) + 32 * REP * i)
                for h in range(2):
                    sp.dma_start(q2[SH * h + SR:SH * h + SR + MR, n, :, :],
                                 max_rows[n, :, h].rearrange("a m s -> m a s")).then_inc(rows_in[n], 16)

            def send_heads(k, g_dyn, i):
                sp.wait_ge(pv_read, k + 1 + 4 * i)
                for j in range(REP):
                    sp.dma_start(heads_out.rearrange("g r d s -> (g r) d s")[
                        bass.ds(g_dyn * REP + j, 1), :, (k % 2) * BLK:(k % 2 + 1) * BLK].rearrange("o d s -> (o d) s"),
                        heads[32 * j:32 * j + D + 1, k % 2, :]).then_inc(heads_free[k % 2], 16)

            def load_heads(c):
                g0, g1, half = PIECES[c]
                for n in range(2):
                    if half is None or half == n:
                        sp.wait_ge(heads_free[n], 16 * REP * (g1 + 1))
                for k0 in range(g0, g1, KV // KE):
                    k1_ = min(g1, k0 + KV // KE)
                    a, b, rows, at = piece_place(k0, k1_, half)
                    src = heads_out.rearrange("g r d s -> (g r) d s")[k0 * REP:k1_ * REP, :, at]
                    to = slice(b * S + at.start, b * S + at.stop)
                    sp.dma_start(attnT[rows, a, to], src[:, 0:D, :]).then_inc(attn_in[c], 16)
                    sp.dma_start(denT[rows, a, to], src[:, D:D + 1, :].to_broadcast(
                        ((k1_ - k0) * REP, D, at.stop - at.start))).then_inc(attn_in[c], 16)

            def first_loads(_):
                for r in (3, 4):
                    sp.wait_ge(stacked[r % 2], stored(r))
                sp.wait_ge(filled, 4)
                load_stacks(q1, k1, 0, 0, qk1_in[0])
                load_stacks(q1, k1, 1, 1, qk1_in[1])
                load_stacks(q2, k2, 0, 0, qk2_in[0])

            ahead(rest=store_parts, comb=comb_out, loads=first_loads)
            for r in (ROPES - 2, ROPES - 1):
                sp.wait_ge(stacked[r % 2], stored(r))
            maxima_rows(0, 0, 0)

            def one(t, i):
                g, s = t // STEPS, t % STEPS
                gd = g + 2 * i
                if place(t) == 1:
                    sp.wait_ge(hid_steps, HID + HID * i)
                    load_mix(i + 1)
                if s == 1 and g >= 1:
                    send_heads(2 * g - 1, gd - 1, i)
                if s == 4:
                    if g + 1 < G:
                        sp.wait_ge(s_ready, entries(g * STEPS) + (2 * LSTEPS + 2) * i)
                        load_stacks(q2, k2, gd + 1, (g + 1) % 2, qk2_in[(g + 1) % 2])
                    if g + 2 < G:
                        sp.wait_ge(m_ready, UNITS * (g + 1) + 2 * UNITS * i)
                        load_stacks(q1, k1, gd + 2, g % 2, qk1_in[g % 2])
                if s == 11:
                    send_heads(2 * g, gd, i)
                if s == 15 and g + 1 < G:
                    maxima_rows(g + 1, (g + 1) % 2, i)
                for c, at in enumerate(PIECE_STEPS):
                    if t == at:
                        if c == 0:
                            sp.wait_ge(res_done, TURNS + 1)
                        load_heads(c)

            steps(sp, one)
            send_heads(2 * G - 1, G - 1, 0)

            load_heads(4)
            ov = out.rearrange("(t p) e -> p t e", p=P)
            for q in range(NBLK):
                sp.wait_ge(o_done, TB * (q + 1))
                sp.dma_start(ov[:, q * TB:(q + 1) * TB, :], res[:, q * TB:(q + 1) * TB, :]).then_inc(out_sent, 16)
            sp.wait_ge(out_sent, 16 * NBLK)

        @block.gpsimd
        def _(pool):
            for n in range(2):
                pool.sem_inc(heads_free[n], 16 * REP)
            pool.memset(q1[:, :, :, :], 0.0).then_inc(filled, 1)
            pool.memset(q2[:, :, :, :], 0.0).then_inc(filled, 1)
            pool.memset(k1[:, :, :], 1.0).then_inc(filled, 1)
            pool.memset(k2[:, :, :], 1.0).then_inc(filled, 1)
            pool.memset(v_now[:, :, :, :], 1.0).then_inc(filled, 1)
            pool.memset(zeros[:, :], 0.0).then_inc(filled, 1)

            def rope_add(r):
                pool.wait_ge(qk_read, 2 * (r + 1))
                pool.tensor_tensor(rope_a[r % 2], rope_a[r % 2], rope_b[r % 2], ALU.add).then_inc(rope_sum, 1)

            def third_part(r):
                pool.wait_ge(part2, r + 1)
                pool.tensor_tensor(parts[:, r % 2, 2, :], rope_b[r % 2], parts[:, r % 2, 1, :], ALU.subtract
                                   ).then_inc(part3, 1)

            def hidden(blk, m, i):
                done, grow = HID * blk + hid_count(m), HID * i
                o = m % GU
                th, gate, up = gu[:, o, 0, :], gu[:, o, 1, :], gu[:, o, 2, :]
                pool.wait_ge(gu_kept, 2 * (FT * blk + m + 1) + 2 * FT * i)
                pool.tensor_tensor(th, th, gate, ALU.mult).then_inc(hid_steps, 1)
                pool.wait_ge(hid_steps, done + 1 + grow)
                pool.tensor_tensor(th, th, gate, ALU.add).then_inc(hid_steps, 1)
                pool.wait_ge(hid_steps, done + 2 + grow)
                if m == 0 and blk >= 1:
                    pool.wait_ge(down_done, blk + i)
                pool.tensor_tensor(hid[:, m, :], th, up, ALU.mult).then_inc(hid_steps, 1)
                if m >= 2:
                    if m == 2:
                        pool.wait_ge(mix_in, 16 * (blk + 1) + 16 * i)
                    pool.wait_ge(hid_steps, done + 3 + grow)
                    pool.tensor_tensor(hid[:, m, :], hid[:, m, :], mix[:, m - 2, :], ALU.mult).then_inc(hid_steps, 1)

            def values(g, n):
                v = v_all[:, :, :, :, :].rearrange("p b k t d -> p (b k) t d")[:, bass.ds(g, 1), :, :].rearrange(
                    "p o t d -> p (o t) d")
                pool.tensor_tensor(v_now[:, n, :, 0:D], v,
                                   zeros[:, 0:KT * D].rearrange("p (t d) -> p t d", t=KT), ALU.add).then_inc(v_ready, 1)

            def split_maxima(g, i):
                ent = turn_entry(g) + 1
                pool.wait_ge(s_done, ent + (2 * LSTEPS + 2) * i)
                if g > 0:
                    pool.wait_ge(rows_stored, 16 * REP * g + 32 * REP * i)
                pool.tensor_tensor(neg_parts[:, 0, :], neg_maxT[:, :], zeros[0:REP * KT, :], ALU.add
                                   ).then_inc(rest_done, 1)
                pool.wait_ge(rest_done, 3 * g + 1 + 6 * i)
                pool.tensor_tensor(neg_parts[:, 1, :], neg_maxT[:, :], neg_parts[:, 0, :], ALU.subtract
                                   ).then_inc(rest_done, 1)
                pool.tensor_tensor(neg_rest[:, :], neg_maxT[:, :], neg_parts[:, 0, :], ALU.subtract
                                   ).then_inc(rest_done, 1)
                pool.wait_ge(rest_done, 3 * g + 3 + 6 * i)
                pool.tensor_tensor(neg_parts[:, 2, :], neg_rest[:, :], neg_parts[:, 1, :], ALU.subtract
                                   ).then_inc(parts_ready, 1)

            def hidden_ahead(j):
                if j % UP_MM == UP_MM - 1 and j < UP_MM * FT:
                    hidden(0, j // UP_MM, 0)

            ahead(rope=rope_add, rest=third_part, f=hidden_ahead)
            pool.wait_ge(vr_read, 2 * NBLK)
            pool.wait_ge(filled, 6)
            values(0, 0)
            split_maxima(0, 0)

            def one(t, i):
                g, s = t // STEPS, t % STEPS
                if s == 3 and g + 1 < G:
                    if g >= 1:
                        pool.wait_ge(pv_done, STEPS * g + LSTEPS * i)
                    values(g + 1 + 2 * i, (g + 1) % 2)
                if s == STEPS - LEAD + 1 and g + 1 < G:
                    split_maxima(g + 1, i)
                if place(t) is not None and place(t) % 2 and 3 <= place(t) <= 2 * FT + 1:
                    hidden(1, (place(t) - 3) // 2, i)

            steps(pool, one)

        @block.scalar
        def _(act):
            act.dma_start(w_qk[:, :, :, :], wqkv).then_inc(w_qk_in, 16)
            act.dma_start(w_vr[:, :, :], wvr).then_inc(w_qk_in, 16)
            act.dma_start(ident[:, :], tables[:, 0:P]).then_inc(tables_in, 16)
            act.dma_start(before[:, :], tables[:, P:P + EXP * EXP]).then_inc(tables_in, 16)
            at = P + EXP * EXP
            act.dma_start(cos_sin[:, :, :], tables[:, at:at + 2 * S].rearrange("p (c s) -> p c s", c=2)
                          ).then_inc(tables_in, 16)
            act.dma_start(cos_sin_k[:, :, :], tables[:, at + 2 * S:].rearrange("p (c s) -> p c s", c=2)
                          ).then_inc(tables_in, 16)

            def root(q):
                act.wait_ge(var_ready, q + 1)
                act.activation(ln[:, 1, q * TB:(q + 1) * TB], ln[:, 0, q * TB:(q + 1) * TB], ACT.Sqrt
                               ).then_inc(root_ready, 1)

            def keep_turned(q):
                act.wait_ge(turned, 2 * q + 1)
                act.activation(xnT[:, 0, q * BLK:(q + 1) * BLK], pb(4), ACT.Copy).then_inc(turned_a, 1)

            def first_part(r):
                act.wait_ge(rope_sum, r + 1)
                if r >= 2:
                    act.wait_ge(stacked[r % 2], stored(r - 2))
                act.activation(parts[:, r % 2, 0, :], rope_a[r % 2], ACT.Copy).then_inc(part1, 1)

            def second_part(r):
                act.wait_ge(rest1, r + 1)
                act.activation(parts[:, r % 2, 1, :], rope_b[r % 2], ACT.Copy).then_inc(part2, 1)

            def keep_vr(q):
                act.wait_ge(vr_ready, q + 1)
                vr = pb(6)[:, 0:TB * (KV * D + EXP)].rearrange("p (t c) -> p t c", t=TB)
                b, t0 = q // QH, (q % QH) * TB
                act.activation(v_all[:, b, :, t0:t0 + TB, :].rearrange("p k t d -> p t k d"),
                               vr[:, :, 0:KV * D].rearrange("p t (k d) -> p t k d", k=KV), ACT.Copy
                               ).then_inc(vr_read, 1)
                act.activation(logits[:, q * TB:(q + 1) * TB, :], vr[:, :, KV * D:], ACT.Copy).then_inc(vr_read, 1)

            def router_exp(_):
                act.wait_ge(top_max, 1)
                act.activation(rt[:, 1, :, :], rt[:, 0, :, :], ACT.Exp).then_inc(top_exp, 1)

            def keep_comb(_):
                act.wait_ge(comb_turned, 1)
                act.activation(combT[:, :], pb(6)[:, 0:P], ACT.Copy).then_inc(comb_kept, 1)

            def keep_gu(blk, m, i):
                o = m % GU
                act.wait_ge(gu_ready, FT * blk + m + 1 + FT * i)
                if m >= GU:
                    act.wait_ge(hid_steps, HID * blk + hid_count(m - GU + 1) + HID * i)
                elif blk >= 1:
                    act.wait_ge(hid_steps, HID * blk + HID * i)
                act.activation(gu[:, o, 0, :], pb(7)[:, 0:FBLK], ACT.Tanh, scale=0.5).then_inc(gu_kept, 1)
                act.activation(gu[:, o, 1:3, :], pb(7).rearrange("p (w n) -> p w n", w=2), ACT.Copy, scale=0.5
                               ).then_inc(gu_kept, 1)

            def gu_ahead(j):
                if j % UP_MM == UP_MM - 1 and j < UP_MM * FT:
                    keep_gu(0, j // UP_MM, 0)

            ahead(norm=root, turn=keep_turned, rope=first_part, rest=second_part, vr=keep_vr, router=router_exp,
                  comb=keep_comb, f=gu_ahead)

            def turned_maxima(g, i):
                ent = turn_entry(g)
                act.wait_ge(s_ready, ent + 1 + (2 * LSTEPS + 2) * i)
                if g > 0:
                    act.wait_ge(parts_ready, g + 2 * i)
                act.activation(neg_maxT[:, :], s_slot(ent)[0:REP * KT, 0:P], ACT.Copy).then_inc(s_done, 1)

            turned_maxima(0, 0)

            def keep_heads(k, i):
                act.wait_ge(pv_done, KT * (k + 1) + LSTEPS * i)
                act.wait_ge(heads_free[k % 2], 16 * REP * (k // 2 + 1) + 32 * REP * i)
                act.activation(heads[:, k % 2, :], pb(6), ACT.Copy).then_inc(pv_read, 1)

            def one(t, i):
                g, s = t // STEPS, t % STEPS
                for n in (2 * t, 2 * t + 1):
                    act.wait_ge(s_ready, pair_entry(n) + 1 + (2 * LSTEPS + 2) * i)
                    if n % 2 == 0 and n >= PSLOTS:
                        act.wait_ge(pv_done, (n - PSLOTS) // 2 + 1 + LSTEPS * i)
                    act.activation(probs[:, n % PSLOTS, :], s_slot(pair_entry(n))[:, :], ACT.Exp, scale=SCALE
                                   ).then_inc(s_done, 1)
                    if n % 2 == 0 and place(t) is not None and place(t) % 2 == 0 and 2 <= place(t) <= 2 * FT:
                        keep_gu(1, (place(t) - 2) // 2, i)
                    if n % 2 == 1 and t >= KT and t % KT == 0:
                        keep_heads(t // KT - 1, i)
                if s == STEPS - LEAD and g + 1 < G:
                    turned_maxima(g + 1, i)

            act.wait_ge(part3, ROPES)
            steps(act, one)
            keep_heads(2 * G - 1, 0)

        @block.vector
        def _(dve):
            chain = [0]

            def link(ins):
                chain[0] += 1
                ins.then_inc(vec, 1)
                dve.wait_ge(vec, chain[0])

            def norm(q):
                sl = slice(q * TB, (q + 1) * TB)
                dve.wait_ge(x_in[q], 16)
                for t in range(q * TB, (q + 1) * TB):
                    last = nc.vector.bn_stats(stats[:, t, :], res[:, t, :])
                link(last)
                for t in range(q * TB, (q + 1) * TB):
                    last = nc.vector.bn_aggr(mv[:, t, :], stats[:, t, :])
                link(last)
                nc.vector.tensor_scalar(ln[:, 0, sl], mv[:, sl, 1], EPS, None, ALU.add).then_inc(var_ready, 1)
                dve.wait_ge(root_ready, q + 1)
                link(nc.vector.reciprocal(ln[:, 2, sl], ln[:, 1, sl]))
                link(nc.vector.tensor_tensor(ln[:, 3, sl], ln[:, 2, sl], ln[:, 2, sl], ALU.mult))
                link(nc.vector.tensor_tensor(ln[:, 1, sl], ln[:, 3, sl], ln[:, 0, sl], ALU.mult))
                link(nc.vector.tensor_scalar(ln[:, 3, sl], ln[:, 1, sl], -0.5, 1.5, ALU.mult, ALU.add))
                link(nc.vector.tensor_tensor(ln[:, 1, sl], ln[:, 2, sl], ln[:, 3, sl], ALU.mult))
                for t in range(q * TB, (q + 1) * TB):
                    nc.vector.tensor_scalar(xn[:, t, :], res[:, t, :], mv[:, t, 0:1], ln[:, 1, t:t + 1],
                                            ALU.subtract, ALU.mult).then_inc(xn_ready, 1)

            def keep_turned(q):
                dve.wait_ge(turned, 2 * q + 2)
                nc.vector.tensor_copy(xnT[:, 1, q * BLK:(q + 1) * BLK], pb(5)).then_inc(turned_d, 1)

            def rope_products(r):
                kind, a, q = ROPE[r]
                tab = cos_sin_k[:, :, :] if kind == "k" else cos_sin[:, :, (q % QH) * BLK:(q % QH + 1) * BLK]
                if r == 0:
                    dve.wait_ge(tables_in, 64)
                dve.wait_ge(qk_ready, r + 1)
                if r >= 2:
                    dve.wait_ge(part3, r - 1)
                nc.vector.tensor_tensor(rope_a[r % 2], pb(2 * (r % 2)), tab[:, 0, :], ALU.mult).then_inc(qk_read, 1)
                nc.vector.tensor_tensor(rope_b[r % 2], pb(2 * (r % 2) + 1), tab[:, 1, :], ALU.mult
                                        ).then_inc(qk_read, 1)

            def first_rest(r):
                dve.wait_ge(part1, r + 1)
                nc.vector.tensor_tensor(rope_b[r % 2], rope_a[r % 2], parts[:, r % 2, 0, :], ALU.subtract
                                        ).then_inc(rest1, 1)

            def router(_):
                dve.wait_ge(vr_read, 2 * NBLK)
                link(nc.vector.tensor_reduce(rs[:, 0, :], logits[:, :, :], AX.X, ALU.max))
                nc.vector.tensor_tensor(rt[:, 0, :, :], logits[:, :, :],
                                        rs[:, 0, :].unsqueeze(2).to_broadcast((P, NT, EXP)), ALU.subtract
                                        ).then_inc(top_max, 1)
                dve.wait_ge(top_exp, 1)
                link(nc.vector.tensor_reduce(rs[:, 0, :], rt[:, 1, :, :], AX.X, ALU.add))
                link(nc.vector.reciprocal(rs[:, 1, :], rs[:, 0, :]))
                link(nc.vector.tensor_tensor(rt[:, 0, :, :], rt[:, 1, :, :],
                                             rs[:, 1, :].unsqueeze(2).to_broadcast((P, NT, EXP)), ALU.mult))
                pj = rt[:, 0, :, :].unsqueeze(2).to_broadcast((P, NT, EXP, EXP))
                pe_ = rt[:, 0, :, :].unsqueeze(3).to_broadcast((P, NT, EXP, EXP))
                nc.vector.tensor_tensor(rank[:, 0], pj, pe_, ALU.is_gt)
                link(nc.vector.tensor_tensor(rank[:, 1], pj, pe_, ALU.is_equal))
                link(nc.vector.tensor_tensor(
                    rank[:, 1], rank[:, 1],
                    before[:, :].rearrange("p (o e j) -> p o e j", o=1, e=EXP).to_broadcast((P, NT, EXP, EXP)), ALU.mult))
                link(nc.vector.tensor_tensor(rank[:, 0], rank[:, 0], rank[:, 1], ALU.add))
                link(nc.vector.tensor_reduce(rt[:, 1, :, :], rank[:, 0], AX.X, ALU.add))
                nc.vector.scalar_tensor_tensor(comb[:, :, :].rearrange("p e t -> p t e"), rt[:, 1, :, :], 2.0,
                                               rt[:, 0, :, :], ALU.is_lt, ALU.mult).then_inc(comb_ready, 1)

            def add_down(i):
                dve.wait_ge(down_done, i + 1)
                r = res[:, bass.ds(i * FTB, FTB), :].rearrange("p t e -> p (t e)")
                nc.vector.scalar_tensor_tensor(r, pb(7), 2.0, r, ALU.mult, ALU.add).then_inc(res_done, 1)

            def unit(m, i):
                g, u = m // UNITS, m % UNITS
                qt, kh, h = unit_of(u)
                if u == 0 and g >= 2:
                    dve.wait_ge(neg_ready, g - 1 + 2 * i)
                dve.wait_ge(m_ready, m + 1 + 2 * UNITS * i)
                col = (h * KT + qt) * 2 + kh
                nc.vector.tensor_reduce(unit_max[:, g % 2, col:col + 1], pb(m_bank(m)), AX.X, ALU.max
                                        ).then_inc(m_done, 1)
                if u == UNITS - 1:
                    dve.wait_ge(m_done, m + 1 + 2 * UNITS * i)
                    if g >= 1:
                        dve.wait_ge(s_ready, turn_entry(g - 1) + 1 + (2 * LSTEPS + 2) * i)
                    nc.vector.tensor_reduce(neg_max[:, g % 2, :],
                                            unit_max[:, g % 2, :].rearrange("p (c k) -> p c k", k=2), AX.X, ALU.max,
                                            negate=True).then_inc(neg_ready, 1)

            ahead(norm=norm, turn=keep_turned, rope=rope_products, rest=first_rest, router=router,
                  m=lambda m: unit(m, 0))

            def one(t, i):
                if place(t) == 0:
                    add_down(i)
                elif t == ROT + TURNS * LSTEPS:
                    add_down(TURNS)
                for m in range(AHEAD + UPS * t, AHEAD + UPS * (t + 1)):
                    if m < G * UNITS:
                        unit(m, i)

            steps(dve, one)

            divided = 0
            for c, (g0, g1, half) in enumerate(PIECES):
                places = [piece_place(k0, min(g1, k0 + 4), half) for k0 in range(g0, g1, 4)]
                dve.wait_ge(attn_in[c], 32 * len(places))
                for a, b, rows, at in places:
                    to = slice(b * S + at.start, b * S + at.stop)
                    nc.vector.reciprocal(denT[rows, a, to], denT[rows, a, to]).then_inc(den_done, 1)
                    divided += 1
                    dve.wait_ge(den_done, divided)
                    nc.vector.tensor_tensor(attnT[rows, a, to], attnT[rows, a, to], denT[rows, a, to], ALU.mult
                                            ).then_inc(attn_done, 1)
            for t in range(NT):
                dve.wait_ge(o_ready, t + 1)
                nc.vector.tensor_tensor(res[:, t, :], pb(t % 8)[:, 0:E], res[:, t, :], ALU.add).then_inc(o_done, 1)

        @block.tensor
        def _(pe):
            pe.wait_ge(tables_in, 64)

            def turn(q):
                pe.wait_ge(xn_ready, TB * (q + 1))
                if q >= 1:
                    pe.wait_ge(turned_a, q)
                    pe.wait_ge(turned_d, q)
                for k in range(KE):
                    for t in range(TB):
                        last = nc.tensor.transpose(pb(4 + k)[:, t * P:(t + 1) * P],
                                                   xn[:, q * TB + t, k * P:(k + 1) * P], ident[:, :])
                    last.then_inc(turned, 1)

            def project(r):
                kind, a, q = ROPE[r]
                if r == 0:
                    pe.wait_ge(w_qk_in, 32)
                blocks = (q + 1) if kind == "q" else QH * (a + 1)
                pe.wait_ge(turned_a, blocks)
                pe.wait_ge(turned_d, blocks)
                if r >= 2:
                    pe.wait_ge(qk_read, 2 * (r - 1))
                for rot in range(2):
                    to = pb(2 * (r % 2) + rot)
                    for k in range(KE):
                        if kind == "q":
                            last = nc.tensor.matmul(to, w_qk[:, k, rot, a * P:(a + 1) * P],
                                                    xnT[:, k, q * BLK:(q + 1) * BLK], start=(k == 0), stop=(k == KE - 1))
                        else:
                            for half in range(2):
                                tok = a * S + half * BLK
                                last = nc.tensor.matmul(to[half * SH:(half + 1) * SH, :],
                                                        w_qk[:, k, rot, 2 * P:2 * P + SH], xnT[:, k, tok:tok + BLK],
                                                        start=(k == 0), stop=(k == KE - 1))
                last.then_inc(qk_ready, 1)

            def values_router(q):
                pe.wait_ge(turned_a, q + 1)
                pe.wait_ge(turned_d, q + 1)
                if q >= 1:
                    pe.wait_ge(vr_read, 2 * q)
                C = KV * D + EXP
                for t in range(TB):
                    for k in range(KE):
                        last = nc.tensor.matmul(pb(6)[:, t * C:(t + 1) * C],
                                                xnT[:, k, q * BLK + t * P:q * BLK + (t + 1) * P],
                                                w_vr[:, k, :], start=(k == 0), stop=(k == KE - 1))
                last.then_inc(vr_ready, 1)

            def turn_comb(_):
                pe.wait_ge(comb_ready, 1)
                pe.wait_ge(vr_read, 2 * NBLK)
                nc.tensor.transpose(pb(6)[:, 0:P], comb[:, :, :].rearrange("p e t -> p (e t)"), ident[:, :]
                                    ).then_inc(comb_turned, 1)

            def feed_forward(blk, j, i):
                if j < UP_MM * FT:
                    m, w, k = j // UP_MM, j % UP_MM // KE, j % KE
                    if m == 0 and j == 0:
                        if blk == 0:
                            pe.wait_ge(w_gu_in, 16)
                        else:
                            pe.wait_ge(res_done, blk + i)
                    elif j % UP_MM == 0:
                        pe.wait_ge(gu_kept, 2 * (FT * blk + m) + 2 * FT * i)
                    mm = nc.tensor.matmul(pb(7)[:, w * FBLK:(w + 1) * FBLK], w_gu[:, k, m, w, :],
                                          xnT[:, k, bass.ds((blk + i) * FBLK, FBLK)], start=(k == 0), stop=(k == KE - 1))
                    if j % UP_MM == UP_MM - 1:
                        mm.then_inc(gu_ready, 1)
                elif j >= DOWN_AT:
                    tt, m = (j - DOWN_AT) // FT, (j - DOWN_AT) % FT
                    if j == DOWN_AT:
                        if blk == 0:
                            pe.wait_ge(w_dn_in, 16)
                        pe.wait_ge(gu_kept, 2 * FT * (blk + 1) + 2 * FT * i)
                    if tt == 0:
                        pe.wait_ge(hid_steps, HID * blk + hid_count(m + 1) + HID * i)
                    mm = nc.tensor.matmul(pb(7)[:, tt * E:(tt + 1) * E], hid[:, m, tt * P:(tt + 1) * P],
                                          w_dn[:, m, :], start=(m == 0), stop=(m == FT - 1))
                    if j == SLOTS - 1:
                        mm.then_inc(down_done, 1)

            def unit(m, i):
                g, u = m // UNITS, m % UNITS
                qt, kh, h = unit_of(u)
                n = g % 2
                if u == 0:
                    pe.wait_ge(qk1_in[n], 96 * (g // 2 + 1) + 96 * i)
                if m >= 2:
                    pe.wait_ge(m_done, m - 1 + 2 * UNITS * i)
                else:
                    pe.wait_ge(turned_a, NBLK)
                    pe.wait_ge(turned_d, NBLK)
                rows = slice(SH * (h % 2), SH * (h % 2) + SH)
                nc.tensor.matmul(pb(m_bank(m)), q1[rows, n, h // 2, qt * P:(qt + 1) * P],
                                 k1[rows, n, kh * BLK:(kh + 1) * BLK], start=True, stop=True).then_inc(m_ready, 1)

            def turn_maxima(g, i):
                ent = turn_entry(g)
                pe.wait_ge(neg_ready, g + 1 + 2 * i)
                if ent >= 2:
                    pe.wait_ge(s_done, ent - 1 + (2 * LSTEPS + 2) * i)
                nc.tensor.transpose(s_slot(ent)[0:REP * KT, 0:P], neg_max[:, g % 2, :], ident[:, :]).then_inc(s_ready, 1)

            def scores(n, i):
                g, s = n // 2 // STEPS, n // 2 % STEPS
                qh, kt = s // KT, s % KT
                e = pair_entry(n)
                if e >= 2:
                    pe.wait_ge(s_done, e - 1 + (2 * LSTEPS + 2) * i)
                for h in range(2):
                    rows = slice(SH * h, SH * h + SH)
                    last = nc.tensor.matmul(s_slot(e)[:, h * BLK:(h + 1) * BLK], k2[rows, g % 2, kt * P:(kt + 1) * P],
                                            q2[rows, g % 2, n % 2, qh * BLK:(qh + 1) * BLK], start=True, stop=True)
                last.then_inc(s_ready, 1)

            def weigh_values(t, i):
                g, kt, k = t // STEPS, t % KT, t // KT
                if kt == 0 and k >= 1:
                    pe.wait_ge(pv_read, k + 4 * i)
                if t % STEPS == 0:
                    pe.wait_ge(v_ready, g + 1 + 2 * i)
                pe.wait_ge(s_done, pair_entry(2 * t + 1) + 1 + (2 * LSTEPS + 2) * i)
                for h in range(REP):
                    n = 2 * t + h // 2
                    last = nc.tensor.matmul(pb(6)[32 * h:32 * h + 32, :], v_now[:, g % 2, kt, :],
                                            probs[:, n % PSLOTS, (h % 2) * BLK:(h % 2 + 1) * BLK],
                                            start=(kt == 0), stop=(kt == KT - 1))
                last.then_inc(pv_done, 1)

            ahead(turn=turn, rope=project, vr=values_router, comb=turn_comb, m=lambda m: unit(m, 0),
                  f=lambda j: feed_forward(0, j, 0))
            pe.wait_ge(qk_read, 2 * ROPES)
            pe.wait_ge(comb_kept, 1)
            turn_maxima(0, 0)

            def one(t, i):
                g, s = t // STEPS, t % STEPS
                if s == 0:
                    pe.wait_ge(qk2_in[g % 2], 96 * (g // 2 + 1) + 96 * i)
                    pe.wait_ge(rows_in[g % 2], 32 * (g // 2 + 1) + 32 * i)
                scores(2 * t, i)
                scores(2 * t + 1, i)
                for n in range(2):
                    for m in range(AHEAD + UPS * t + 2 * n, AHEAD + UPS * t + 2 * n + 2):
                        if m < G * UNITS:
                            unit(m, i)
                    if n == 0 and t >= 1:
                        weigh_values(t - 1, i)
                    if place(t) is not None:
                        feed_forward(1, 2 * place(t) + n, i)
                if s == STEPS - LEAD and g + 1 < G:
                    turn_maxima(g + 1, i)

            steps(pe, one)
            weigh_values(G * STEPS - 1, 0)

            pe.wait_ge(w_o_in, 16)
            for t in range(NT):
                if t == 0:
                    pe.wait_ge(pv_read, 2 * G)
                    pe.wait_ge(m_done, G * UNITS)
                    pe.wait_ge(s_done, entries(G * STEPS))
                    pe.wait_ge(res_done, TURNS + 1)
                if t >= 8:
                    pe.wait_ge(o_done, t - 7)
                if t % TB == 0:
                    pe.wait_ge(attn_done, (2, 2, 5, 6)[t // TB])
                for a in range(KE):
                    last = nc.tensor.matmul(pb(t % 8)[:, 0:E], attnT[:, a, t * P:(t + 1) * P], w_o[:, a, :],
                                            start=(a == 0), stop=(a == KE - 1))
                last.then_inc(o_ready, 1)


def kernel(L0_attn_x, L0_attn_Wq, L0_attn_Wk, L0_attn_Wv, L0_attn_Wo, L0_ffn_router_w, L0_ffn_shared_gate,
           L0_ffn_shared_up, L0_ffn_shared_down, L0_ffn_w_gate, L0_ffn_w_up, L0_ffn_w_down):
    import concourse.bacc as bacc
    from concourse.bass_utils import run_bass_kernel_spmd

    def a(v):
        return np.asarray(v)

    swap = np.arange(E).reshape(-1, 2, HALF)[:, ::-1].reshape(-1)
    wq, wk, wv = a(L0_attn_Wq), a(L0_attn_Wk), a(L0_attn_Wv)
    plain = np.concatenate([wq, wk])
    other = np.concatenate([wq[swap], wk[swap[:KV * D]]])
    wqkv = np.stack([plain.T, other.T], 1).reshape(KE, P, 2, -1).transpose(1, 0, 2, 3)
    wvr = np.concatenate([wv.T, a(L0_ffn_router_w)], 1).reshape(KE, P, -1).transpose(1, 0, 2)
    wo = a(L0_attn_Wo).T.reshape(KE, P, E).transpose(1, 0, 2)
    sg, su, eg, eu = a(L0_ffn_shared_gate), a(L0_ffn_shared_up), a(L0_ffn_w_gate), a(L0_ffn_w_up)
    gate = np.concatenate([sg, eg.transpose(1, 0, 2).reshape(E, -1)], 1).reshape(E, FT, P)
    up = np.concatenate([su, eu.transpose(1, 0, 2).reshape(E, -1)], 1).reshape(E, FT, P)
    wgu = np.stack([gate, up], 2).reshape(KE, P, FT, 2, P).transpose(1, 0, 2, 3, 4)
    wdn = np.concatenate([a(L0_ffn_shared_down).reshape(2, P, E), a(L0_ffn_w_down)]).transpose(1, 0, 2)

    f = np.float32
    inv = (f(1.0) / np.power(f(10000.0), np.arange(0, D, 2, dtype=f) / f(D))).astype(f)
    angle = np.outer(np.arange(S, dtype=f), inv).astype(f)
    cos = np.cos(angle).T[np.arange(P) % HALF]
    sin = np.sin(angle).T[np.arange(P) % HALF]
    sign = np.where(np.arange(P) % D < HALF, f(-1), f(1))[:, None]
    before = np.broadcast_to(np.tril(np.ones((EXP, EXP), f), -1).reshape(1, -1), (P, EXP * EXP))
    stack = [np.concatenate([v[:SH, :BLK], v[:SH, BLK:]]) for v in (cos, sin * sign)]
    tables = np.concatenate([np.eye(P, dtype=f), before, cos, sin * sign, *stack], 1).astype(f)

    arrays = {"x": a(L0_attn_x).reshape(N, E), "wqkv": wqkv, "wo": wo, "wgu": wgu, "wdn": wdn, "wvr": wvr,
              "tables": tables}
    arrays = {k: np.ascontiguousarray(v) for k, v in arrays.items()}
    nc = bacc.Bacc("TRN2", target_bir_lowering=False, num_devices=1)
    aps = {k: nc.dram_tensor(k, v.shape, mybir.dt.from_np(v.dtype), kind="ExternalInput").ap()
           for k, v in arrays.items()}
    out = nc.dram_tensor("out", (N, E), F32, kind="ExternalOutput").ap()
    ffn_attention_block(nc, out=out, **aps)
    r = run_bass_kernel_spmd(nc, [arrays], core_ids=[0])
    return r.results[0]["out"].reshape(B, S, E)
```

```python
from contextlib import ExitStack

import numpy as np

import concourse.bass as bass
from concourse import mybir

ALU = mybir.AluOpType
ACT = mybir.ActivationFunctionType
AX = mybir.AxisListType
F32 = mybir.dt.float32
BF16 = mybir.dt.bfloat16

P = 128
B, S, E = 2, 1024, 256
H, KV = 32, 8
D = E // H
REP = H // KV
N = B * S
KE = E // P
BLK = 512
NBLK = N // BLK
TB = BLK // P
NT = N // P
EXP = 8
FT = 2 + EXP
EPS = 1e-5
HALF = D // 2

QPART = (0, 0, 0, 1, 2, 1)
KPART = (2, 1, 0, 0, 0, 1)
NP = len(QPART)
SR = NP * D
MR = 3
SH = 64

G = B * KV
KT = S // P
QH = S // BLK
STEPS = QH * KT
UNITS = REP * (S // P) * (S // BLK)
UPS = UNITS // STEPS
LEAD = 4
AHEAD = UNITS + LEAD * UPS
ROT = 4
LSTEPS = 2 * STEPS
TURNS = (G * STEPS - ROT) // LSTEPS
PSLOTS = 4
VW = 32
SCALE = 1.0 / float(np.sqrt(D))
FBLK = N // (TURNS + 1)
FTB = FBLK // P
UP_MM = 2 * KE
DOWN_AT = UP_MM * FT + 2
SLOTS = DOWN_AT + FT * FTB
GU = 3


def ffn_attention_block(nc, x, wqkv, wo, wgu, wdn, wvr, tables, out):
    ctx = ExitStack()
    with ctx:
        def sb(name, shape, dt=F32):
            return ctx.enter_context(nc.sbuf_tensor(name, shape, dt))

        def sem(name):
            return ctx.enter_context(nc.semaphore(name))

        bank = [ctx.enter_context(nc.psum_tensor(f"bank{n}", [P, 2 * BLK], F32)) for n in range(4)]

        def pb(n):
            return bank[n // 2][:, (n % 2) * BLK:(n % 2 + 1) * BLK]

        q_stacks = nc.dram_tensor("q_stacks", (NP, G * REP * D, S), BF16).ap()
        k_stacks = nc.dram_tensor("k_stacks", (NP, G * D, S), BF16).ap()
        weights_by_expert = nc.dram_tensor("weights_by_expert", (EXP, N), F32).ap()
        max_rows = nc.dram_tensor("max_rows", (2, 2, 2, MR, S), BF16).ap()
        heads_out = nc.dram_tensor("heads_out", (G, REP, D + 1, S), F32).ap()
        inverses = nc.dram_tensor("inverses", ((KV + 4) * REP, S), F32).ap()

        res = sb("res", [P, NT, E])
        xn = sb("xn", [P, NT, E])
        xnT = sb("xnT", [P, KE, N])
        w_gu = sb("w_gu", [P, KE, FT, 2, P])
        w_dn = sb("w_dn", [P, FT, E])
        w_o = sb("w_o", [P, KE, E])
        w_vr = sb("w_vr", [P, KE, KV * D + EXP])
        early = sb("early", [P, 2 * S + 2 * BLK + KE * 2 * (2 * P + SH)])
        ident = sb("ident", [P, P])
        zeros = sb("zeros", [P, P])
        before = sb("before", [P, EXP * EXP])
        mix = sb("mix", [P, EXP, FBLK])
        work = sb("work", [P, FT * FBLK + GU * 3 * FBLK])
        parts = sb("parts", [P, 2, 3, BLK], BF16)
        q1 = sb("q1", [P, 2, 2, S], BF16)
        k1 = sb("k1", [P, 2, S], BF16)
        q2 = sb("q2", [P, 2, 2, S], BF16)
        k2 = sb("k2", [P, 2, S], BF16)
        probs = sb("probs", [P, PSLOTS, 2 * BLK])
        heads = sb("heads", [P, 2, BLK])
        v_all = sb("v_all", [P, B, KV, KT, D])
        v_now = sb("v_now", [P, 2, KT, VW])
        stats = sb("stats", [P, NT, 6])
        mv = sb("mv", [P, NT, 2])
        ln = sb("ln", [P, 4, NT])
        logits = sb("logits", [P, NT, EXP])
        rt = sb("rt", [P, 2, NT, EXP])
        rs = sb("rs", [P, 2, NT])
        comb = sb("comb", [P, EXP, NT])
        combT = sb("combT", [P, P])
        unit_max = sb("unit_max", [P, 2, UNITS])
        neg_max = sb("neg_max", [P, 2, UNITS // 2])
        neg_maxT = sb("neg_maxT", [REP * KT, P])
        neg_rest = sb("neg_rest", [REP * KT, P])
        neg_parts = sb("neg_parts", [REP * KT, MR, P], BF16)
        hid = work[:, 0:FT * FBLK].rearrange("p (m n) -> p m n", m=FT)
        gu = work[:, FT * FBLK:].rearrange("p (o w n) -> p o w n", o=GU, w=3)
        cos_sin = early[:, 0:2 * S].rearrange("p (c s) -> p c s", c=2)
        cos_sin_k = early[:, 2 * S:2 * S + 2 * BLK].rearrange("p (c s) -> p c s", c=2)
        w_qk = early[:, 2 * S + 2 * BLK:].rearrange("p (k r f) -> p k r f", k=KE, r=2)
        attnT = early[:, 0:KE * N].rearrange("p (a n) -> p a n", a=KE)
        xflat = xn[:, :, :].rearrange("p t e -> p (t e)")
        packed = work[0:2 * (KV + 4) * REP, 0:BLK]
        denT = xflat.rearrange("p (a n) -> p a n", a=KE)
        rank = xflat[:, 0:2 * NT * EXP * EXP].rearrange("p (w t e j) -> p w t e j", w=2, t=NT, e=EXP)
        rope_a = [probs[:, n, 0:BLK] for n in range(2)]
        rope_b = [probs[:, n, BLK:2 * BLK] for n in range(2)]

        x_in = [sem(f"x_in{q}") for q in range(NBLK)]
        tables_in, w_qk_in, w_gu_in, w_dn_in = sem("tables_in"), sem("w_qk_in"), sem("w_gu_in"), sem("w_dn_in")
        w_o_in, w_vr_in = sem("w_o_in"), sem("w_vr_in")
        ident_in, tables_k_in, before_in = sem("ident_in"), sem("tables_k_in"), sem("before_in")
        filled = sem("filled")
        vec = sem("vec")
        var_ready, root_ready, scale_ready, xn_ready = (
            sem("var_ready"), sem("root_ready"), sem("scale_ready"), sem("xn_ready"))
        turned, turned_a, turned_d = sem("turned"), sem("turned_a"), sem("turned_d")
        qk_ready, qk_read, rope_sum = sem("qk_ready"), sem("qk_read"), sem("rope_sum")
        part1, rest1, part2, part3 = sem("part1"), sem("rest1"), sem("part2"), sem("part3")
        stacked = [sem(f"stacked{n}") for n in range(2)]
        vr_ready, vr_read = sem("vr_ready"), sem("vr_read")
        top_max, top_exp = sem("top_max"), sem("top_exp")
        comb_ready, comb_turned, comb_kept, comb_stored = (
            sem("comb_ready"), sem("comb_turned"), sem("comb_kept"), sem("comb_stored"))
        mix_in = sem("mix_in")
        gu_ready, gu_tanh, gu_kept, gu_one = sem("gu_ready"), sem("gu_tanh"), sem("gu_kept"), sem("gu_one")
        hid_steps, down_done, res_done = sem("hid_steps"), sem("down_done"), sem("res_done")
        qk1_in = [sem(f"qk1_in{n}") for n in range(2)]
        qk2_in = [sem(f"qk2_in{n}") for n in range(2)]
        m_ready, m_done, neg_ready = sem("m_ready"), sem("m_done"), sem("neg_ready")
        s_ready, s_done = sem("s_ready"), sem("s_done")
        rest_done, parts_ready, rows_stored = sem("rest_done"), sem("parts_ready"), sem("rows_stored")
        rows_in = [sem(f"rows_in{n}") for n in range(2)]
        v_ready, pv_done, pv_read = sem("v_ready"), sem("pv_done"), sem("pv_read")
        heads_free = [sem(f"heads_free{n}") for n in range(2)]
        attn_in = [sem(f"attn_in{c}") for c in range(4)]
        packed_in, packed_out = sem("packed_in"), sem("packed_out")
        den_done, attn_done, o_ready, o_done, out_sent = (
            sem("den_done"), sem("attn_done"), sem("o_ready"), sem("o_done"), sem("out_sent"))

        ROPE = []
        for b in range(B):
            ROPE += [("q", 0, QH * b), ("k", b, None), ("q", 0, QH * b + 1), ("q", 1, QH * b), ("q", 1, QH * b + 1)]
        ROPES = len(ROPE)

        def stored(r):
            return sum(16 * 3 * (1 if ROPE[j][0] == "q" else 2) for j in range(r % 2, r + 1, 2))

        def ffn_place(t):
            if ROT <= t < ROT + TURNS * LSTEPS:
                p = (t - ROT) % LSTEPS
                return p, range(2 * p, min(2 * p + 2, SLOTS))
            return None, ()

        def tile_up(j):
            return [j // UP_MM] if j < UP_MM * FT and j % UP_MM == UP_MM - 1 else []

        def tiles_up(t):
            return [n for j in ffn_place(t)[1] for n in tile_up(j)]

        def steps_before(t, n):
            p = ffn_place(t)[0]
            return t - n if p is not None and p >= n else 0

        def hid_count(m):
            return 2 * m + max(m - 2, 0)

        HID = hid_count(FT)

        NORMS = [(0,), (1,), (2, 3)]
        SCHEDULE = """
            stats0 norm0 turn0 stats1 norm1 plain0 turn1 rope0 stats2 stats3 rest0 other0 plain1 other1 vr0
            plain2 norm2 other2 rope1 rest1 rope2 vr1 rest2 plain3 loads0 turn2 turn3 rope3 other3 plain4 vr2
            other4 units2 rope4 plain5 units1 other5 units1 rest3 rest4 units1 loads1 vr3 units2 rope5 plain6
            router0 units1 other6 units1 rope6 units1 plain7 ffn1 router1 ffn1 rest5 units2 router2 ffn1 rest6
            units1 rope7 ffn1 router3 other7 plain8 other8 units4 ffn1 router4 units1 router5 comb0 rest7 rope8
            units1 ffn1 plain9 units1 other9 ffn1 rope9 units2 ffn1 rest8 ffn1 units1 ffn1 units2 ffn1 units1
            ffn1 units1 ffn1 rest9 units1 ffn1 units2 ffn1 units1 ffn1 units2 ffn1 maxima0 units1 ffn1 units1
            ffn2 units1 ffn1 units1 ffn1 units1 ffn1 units1 ffn2 units1 ffn2
        """
        AHEAD_ORDER, taken = [], {"units": 0, "ffn": 0}
        for word in SCHEDULE.split():
            what = word.rstrip("0123456789")
            n = int(word[len(what):])
            if what in taken:
                AHEAD_ORDER += [(what, j) for j in range(taken[what], taken[what] + 2 * n)]
                taken[what] += 2 * n
            else:
                AHEAD_ORDER.append((what, n))

        UNITS_AT_COMB = sum(what == "units" for what, _ in AHEAD_ORDER[:AHEAD_ORDER.index(("comb", 0))])

        def entries(t):
            return 1 + 2 * t + min((t + LEAD - 1) // STEPS, G - 1)

        def turn_entry(g):
            return 0 if g == 0 else entries(STEPS * g - LEAD) + 2

        def pair_entry(n):
            return entries(n // 2) + n % 2

        def unit_of(u):
            return u // 4 % KT, u // 2 % 2, u // 32 * 2 + u % 2

        THREE = AHEAD // 6 * 6

        def m_bank(m):
            return 4 + m % (3 if m < THREE else 2)

        def vr_bank(q):
            return pb(6 if q == 1 else 7)

        PIECES = [(0, KV + 4, None), (KV + 4, G - 1, None), (G - 1, G, 0), (G - 1, G, 1)]
        LOAD_STEPS = [G * STEPS - 27, G * STEPS - 12, G * STEPS - 6]
        INVERT_STEP = G * STEPS - 20
        PARTS = (1, 4, 1, 4)
        DIVIDE_STEPS = [G * STEPS - 12, G * STEPS - 7, G * STEPS - 2]
        PROJECT_STEP = G * STEPS - 10

        def piece_place(g0, g1, half):
            b, k = g0 // KV, g0 % KV
            rows = slice(k % 4 * REP * D, (k % 4 + g1 - g0) * REP * D)
            return k // 4, b, rows, slice(0, S) if half is None else slice(half * BLK, (half + 1) * BLK)

        def out_bank(t):
            return pb(4 + t % 2 if t < NT // B else t - NT // B)

        def s_slot(e):
            return bank[e % 2]

        def steps(eng, one):
            for t in range(ROT):
                one(t, 0)
            with eng.Fori(0, TURNS) as i:
                for t in range(ROT, ROT + LSTEPS):
                    one(t, i)
            for t in range(ROT + TURNS * LSTEPS, G * STEPS):
                one(t, 0)

        def ahead(**does):
            for what, n in AHEAD_ORDER:
                if what in does:
                    does[what](n)

        block = ctx.enter_context(nc.Block())

        @block.sync
        def _(sp):
            xv = x.rearrange("(t p) e -> p t e", p=P)
            at = P + EXP * EXP

            def load_x(q):
                sp.dma_start(res[:, q * TB:(q + 1) * TB, :], xv[:, q * TB:(q + 1) * TB, :]).then_inc(x_in[q], 16)

            load_x(0)
            sp.dma_start(w_qk[:, :, :, :], wqkv).then_inc(w_qk_in, 16)
            load_x(1)
            sp.dma_start(cos_sin_k[:, :, :], tables[:, at + 2 * S:].rearrange("p (c s) -> p c s", c=2)
                         ).then_inc(tables_k_in, 16)
            load_x(2)
            load_x(3)
            sp.wait_ge(x_in[3], 16)
            sp.dma_start(w_gu[:, :, :, :, :], wgu).then_inc(w_gu_in, 16)
            sp.dma_start(w_dn[:, :, :], wdn).then_inc(w_dn_in, 16)
            sp.dma_start(w_o[:, :, :], wo).then_inc(w_o_in, 16)

            def store_parts(r):
                kind, a, q = ROPE[r]
                sp.wait_ge(part3, r + 1)
                for part in range(3):
                    js = [j for j in range(NP) if (QPART if kind == "q" else KPART)[j] == part]
                    js = slice(js[0], js[-1] + 1, js[1] - js[0] if len(js) > 1 else 1)
                    for half in range(1 if kind == "q" else 2):
                        if kind == "q":
                            f0 = q // QH * E + a * P
                            to = q_stacks[js, f0:f0 + P, (q % QH) * BLK:(q % QH + 1) * BLK]
                            src = parts[:, r % 2, part, :]
                        else:
                            f0 = a * KV * D
                            to = k_stacks[js, f0:f0 + KV * D, half * BLK:(half + 1) * BLK]
                            src = parts[half * SH:(half + 1) * SH, r % 2, part, :]
                        n, rows = to.shape[0], to.shape[1]
                        sp.dma_start(to.rearrange("j f s -> f j s"), src.unsqueeze(1).to_broadcast((rows, n, BLK))
                                     ).then_inc(stacked[r % 2], 16)

            def load_mix(blk):
                sp.dma_start(mix[:, :, :], weights_by_expert[:, bass.ds(blk * FBLK, FBLK)].unsqueeze(0).to_broadcast(
                    (P, EXP, FBLK))).then_inc(mix_in, 16)

            def comb_out(_):
                sp.wait_ge(comb_kept, 1)
                sp.dma_start(weights_by_expert.rearrange("e (t p) -> (e t) p", p=P), combT[:, :]
                             ).then_inc(comb_stored, 16)
                sp.wait_ge(comb_stored, 16)
                load_mix(0)

            def load_stacks(q_to, k_to, g, n, landed):
                for h in range(2):
                    at = SH * h
                    sp.dma_start(q_to[at:at + SR, n, :, :].rearrange("r a s -> r (a s)"),
                                 q_stacks[:, bass.ds(g * REP * D + h * 2 * D, 2 * D), :].rearrange(
                                     "j (d a) s -> j d (a s)", a=2)).then_inc(landed, 16)
                    sp.dma_start(k_to[at:at + SR, n, :], k_stacks[:, bass.ds(g * D, D), :]).then_inc(landed, 16)

            def maxima_rows(g, n, i):
                sp.wait_ge(parts_ready, g + 1 + 2 * i)
                for h in range(REP):
                    sp.dma_start(max_rows[n, h // 2, h % 2].rearrange("m (t p) -> t m p", p=P),
                                 neg_parts[h * KT:(h + 1) * KT, :, :]).then_inc(rows_stored, 16)
                sp.wait_ge(rows_stored, 16 * REP * (g + 1) + 32 * REP * i)
                for h in range(2):
                    sp.dma_start(q2[SH * h + SR:SH * h + SR + MR, n, :, :],
                                 max_rows[n, :, h].rearrange("a m s -> m a s")).then_inc(rows_in[n], 16)

            def send_heads(k, g_dyn, i):
                sp.wait_ge(pv_read, k + 1 + 4 * i)
                for j in range(REP):
                    sp.dma_start(heads_out.rearrange("g r d s -> (g r) d s")[
                        bass.ds(g_dyn * REP + j, 1), :, (k % 2) * BLK:(k % 2 + 1) * BLK].rearrange("o d s -> (o d) s"),
                        heads[32 * j:32 * j + D + 1, k % 2, :]).then_inc(heads_free[k % 2], 16)

            def load_heads(c):
                g0, g1, half = PIECES[c]
                for n in range(2):
                    if half is None or half == n:
                        sp.wait_ge(heads_free[n], 16 * REP * (g1 + 1))
                for k0 in range(g0, g1, KV // KE):
                    k1_ = min(g1, k0 + KV // KE)
                    a, b, rows, at = piece_place(k0, k1_, half)
                    src = heads_out.rearrange("g r d s -> (g r) d s")[k0 * REP:k1_ * REP, :, at]
                    to = slice(b * S + at.start, b * S + at.stop)
                    sp.dma_start(attnT[rows, a, to], src[:, 0:D, :]).then_inc(attn_in[c], 16)
                    if c > 0:
                        sp.dma_start(denT[rows, a, to], src[:, D:D + 1, :].to_broadcast(
                            ((k1_ - k0) * REP, D, at.stop - at.start))).then_inc(attn_in[c], 16)
                if c == 0:
                    sp.wait_ge(res_done, TURNS + 1)
                    sp.dma_start(packed, heads_out.rearrange("g r d s -> (g r) d s")[0:g1 * REP, D, :].rearrange(
                        "r (c s) -> r c s", c=2)).then_inc(packed_in, 16)

            def load_inverses():
                g0, g1, half = PIECES[0]
                sp.wait_ge(den_done, 1)
                sp.dma_start(inverses.rearrange("r (c s) -> r c s", c=2), packed).then_inc(packed_out, 16)
                sp.wait_ge(packed_out, 16)
                for k0 in range(g0, g1, KV // KE):
                    a, b, rows, at = piece_place(k0, k0 + KV // KE, half)
                    sp.dma_start(denT[rows, a, b * S:(b + 1) * S], inverses[
                        k0 * REP:(k0 + KV // KE) * REP, :].unsqueeze(1).to_broadcast((REP * KV // KE, D, S))
                        ).then_inc(attn_in[0], 16)

            def send_out(t0, t1):
                sp.wait_ge(o_done, t1)
                sp.dma_start(out.rearrange("(t p) e -> p t e", p=P)[:, t0:t1, :], res[:, t0:t1, :]
                             ).then_inc(out_sent, 16)

            def first_loads(n):
                if n == 0:
                    for r in (1, 2):
                        sp.wait_ge(stacked[r % 2], stored(r))
                    sp.wait_ge(filled, 4)
                    load_stacks(q1, k1, 0, 0, qk1_in[0])
                else:
                    load_stacks(q1, k1, 1, 1, qk1_in[1])
                    load_stacks(q2, k2, 0, 0, qk2_in[0])

            def first_maxima(_):
                for r in (ROPES - 2, ROPES - 1):
                    sp.wait_ge(stacked[r % 2], stored(r))
                maxima_rows(0, 0, 0)

            ahead(rest=store_parts, comb=comb_out, loads=first_loads, maxima=first_maxima)

            def one(t, i):
                g, s = t // STEPS, t % STEPS
                gd = g + 2 * i
                if ffn_place(t)[0] == 0:
                    sp.wait_ge(hid_steps, HID + HID * i)
                    load_mix(i + 1)
                if s == 1 and g >= 1:
                    send_heads(2 * g - 1, gd - 1, i)
                if s == 4:
                    if g + 1 < G:
                        sp.wait_ge(s_ready, entries(g * STEPS) + (2 * LSTEPS + 2) * i)
                        load_stacks(q2, k2, gd + 1, (g + 1) % 2, qk2_in[(g + 1) % 2])
                    if g + 2 < G:
                        sp.wait_ge(m_ready, UNITS * (g + 1) + 2 * UNITS * i)
                        load_stacks(q1, k1, gd + 2, g % 2, qk1_in[g % 2])
                if s == KT + 1:
                    send_heads(2 * g, gd, i)
                if s == STEPS - LEAD + 1 and g + 1 < G:
                    maxima_rows(g + 1, (g + 1) % 2, i)
                for c, at in enumerate(LOAD_STEPS):
                    if t == at:
                        load_heads(c)
                if t == INVERT_STEP + 1:
                    load_inverses()
                if t == G * STEPS - 2:
                    send_out(0, NT // B)

            steps(sp, one)
            send_heads(2 * G - 1, G - 1, 0)
            load_heads(3)
            send_out(NT // B, NT - TB)
            send_out(NT - TB, NT - 1)
            send_out(NT - 1, NT)
            sp.wait_ge(out_sent, 16 * 4)

        @block.gpsimd
        def _(pool):
            for n in range(2):
                pool.sem_inc(heads_free[n], 16 * REP)
            pool.memset(q1[:, :, :, :], 0.0).then_inc(filled, 1)
            pool.memset(q2[:, :, :, :], 0.0).then_inc(filled, 1)
            pool.memset(k1[:, :, :], 1.0).then_inc(filled, 1)
            pool.memset(k2[:, :, :], 1.0).then_inc(filled, 1)
            pool.memset(v_now[:, :, :, :], 1.0).then_inc(filled, 1)
            pool.memset(zeros[:, :], 0.0).then_inc(filled, 1)

            def rope_add(r):
                pool.wait_ge(qk_read, 2 * (r + 1))
                pool.tensor_tensor(rope_a[r % 2], rope_a[r % 2], rope_b[r % 2], ALU.add).then_inc(rope_sum, 1)

            def third_part(r):
                pool.wait_ge(part2, r + 1)
                pool.tensor_tensor(parts[:, r % 2, 2, :], rope_b[r % 2], parts[:, r % 2, 1, :], ALU.subtract
                                   ).then_inc(part3, 1)

            def hidden(blk, m, i):
                done, grow = HID * blk + hid_count(m), HID * i
                o = m % GU
                th, gate, up = gu[:, o, 0, :], gu[:, o, 1, :], gu[:, o, 2, :]
                pool.wait_ge(gu_kept, FT * blk + m + 1 + FT * i)
                pool.wait_ge(gu_one, FT * blk + m + 1 + FT * i)
                pool.tensor_tensor(th, th, gate, ALU.mult).then_inc(hid_steps, 1)
                pool.wait_ge(hid_steps, done + 1 + grow)
                if m == 0 and blk >= 1:
                    pool.wait_ge(down_done, blk + i)
                pool.tensor_tensor(hid[:, m, :], th, up, ALU.mult).then_inc(hid_steps, 1)
                if m >= 2:
                    if m == 2:
                        pool.wait_ge(mix_in, 16 * (blk + 1) + 16 * i)
                    pool.wait_ge(hid_steps, done + 2 + grow)
                    pool.tensor_tensor(hid[:, m, :], hid[:, m, :], mix[:, m - 2, :], ALU.mult).then_inc(hid_steps, 1)

            def values(g, n):
                v = v_all[:, :, :, :, :].rearrange("p b k t d -> p (b k) t d")[:, bass.ds(g, 1), :, :].rearrange(
                    "p o t d -> p (o t) d")
                pool.tensor_tensor(v_now[:, n, :, 0:D], v,
                                   zeros[:, 0:KT * D].rearrange("p (t d) -> p t d", t=KT), ALU.add).then_inc(v_ready, 1)

            def split_maxima(g, i):
                ent = turn_entry(g) + 1
                pool.wait_ge(s_done, ent + (2 * LSTEPS + 2) * i)
                if g > 0:
                    pool.wait_ge(rows_stored, 16 * REP * g + 32 * REP * i)
                pool.tensor_tensor(neg_parts[:, 0, :], neg_maxT[:, :], zeros[0:REP * KT, :], ALU.add
                                   ).then_inc(rest_done, 1)
                pool.wait_ge(rest_done, 3 * g + 1 + 6 * i)
                pool.tensor_tensor(neg_parts[:, 1, :], neg_maxT[:, :], neg_parts[:, 0, :], ALU.subtract
                                   ).then_inc(rest_done, 1)
                pool.tensor_tensor(neg_rest[:, :], neg_maxT[:, :], neg_parts[:, 0, :], ALU.subtract
                                   ).then_inc(rest_done, 1)
                pool.wait_ge(rest_done, 3 * g + 3 + 6 * i)
                pool.tensor_tensor(neg_parts[:, 2, :], neg_rest[:, :], neg_parts[:, 1, :], ALU.subtract
                                   ).then_inc(parts_ready, 1)

            def first_split(_):
                pool.wait_ge(vr_read, 2 * NBLK)
                pool.wait_ge(filled, 6)
                values(0, 0)
                split_maxima(0, 0)

            def hidden_ahead(j):
                for m in tile_up(j):
                    hidden(0, m, 0)

            ahead(rope=rope_add, rest=third_part, ffn=hidden_ahead, maxima=first_split)

            def one(t, i):
                g, s = t // STEPS, t % STEPS
                if s == 3 and g + 1 < G:
                    if g >= 1:
                        pool.wait_ge(pv_done, STEPS * g + LSTEPS * i)
                    values(g + 1 + 2 * i, (g + 1) % 2)
                if s == STEPS - LEAD + 1 and g + 1 < G:
                    split_maxima(g + 1, i)
                for m in tiles_up(steps_before(t, 2)):
                    hidden(1, m, i)

            steps(pool, one)

        @block.scalar
        def _(act):
            at = P + EXP * EXP
            act.dma_start(ident[:, :], tables[:, 0:P]).then_inc(ident_in, 16)
            act.dma_start(cos_sin[:, :, :], tables[:, at:at + 2 * S].rearrange("p (c s) -> p c s", c=2)
                          ).then_inc(tables_in, 16)
            act.dma_start(w_vr[:, :, :], wvr).then_inc(w_vr_in, 16)
            act.dma_start(before[:, :], tables[:, P:P + EXP * EXP]).then_inc(before_in, 16)

            def normalise(n):
                sl = slice(NORMS[n][0] * TB, (NORMS[n][-1] + 1) * TB)
                act.wait_ge(var_ready, n + 1)
                act.activation(ln[:, 1, sl], ln[:, 0, sl], ACT.Sqrt).then_inc(root_ready, 1)
                act.wait_ge(scale_ready, n + 1)
                for t in range(sl.start, sl.stop):
                    act.activation(xn[:, t, :], res[:, t, :], ACT.Identity, bias=ln[:, 2, t:t + 1],
                                   scale=ln[:, 1, t:t + 1]).then_inc(xn_ready, 1)

            def keep_turned(q):
                act.wait_ge(turned, 2 * q + 1)
                act.activation(xnT[:, 0, q * BLK:(q + 1) * BLK], pb(4), ACT.Copy).then_inc(turned_a, 1)

            def first_part(r):
                act.wait_ge(rope_sum, r + 1)
                if r >= 2:
                    act.wait_ge(stacked[r % 2], stored(r - 2))
                act.activation(parts[:, r % 2, 0, :], rope_a[r % 2], ACT.Copy).then_inc(part1, 1)

            def second_part(r):
                act.wait_ge(rest1, r + 1)
                act.activation(parts[:, r % 2, 1, :], rope_b[r % 2], ACT.Copy).then_inc(part2, 1)

            def keep_vr(q):
                act.wait_ge(vr_ready, q + 1)
                vr = vr_bank(q)[:, 0:TB * (KV * D + EXP)].rearrange("p (t c) -> p t c", t=TB)
                b, t0 = q // QH, (q % QH) * TB
                act.activation(v_all[:, b, :, t0:t0 + TB, :].rearrange("p k t d -> p t k d"),
                               vr[:, :, 0:KV * D].rearrange("p t (k d) -> p t k d", k=KV), ACT.Copy
                               ).then_inc(vr_read, 1)
                act.activation(logits[:, q * TB:(q + 1) * TB, :], vr[:, :, KV * D:], ACT.Copy).then_inc(vr_read, 1)

            def router_exp(stage):
                if stage > 0:
                    return
                act.wait_ge(top_max, 1)
                act.activation(rt[:, 1, :, :], rt[:, 0, :, :], ACT.Exp).then_inc(top_exp, 1)

            def keep_comb(_):
                act.wait_ge(comb_turned, 1)
                act.activation(combT[:, :], pb(6)[:, 0:P], ACT.Copy).then_inc(comb_kept, 1)

            def keep_gu(blk, m, i):
                o = m % GU
                act.wait_ge(gu_ready, FT * blk + m + 1 + FT * i)
                if blk >= 1 or m >= GU:
                    act.wait_ge(hid_steps, HID * blk + (hid_count(m - GU + 1) if m >= GU else 0) + HID * i)
                act.activation(gu[:, o, 0, :], pb(7)[:, 0:FBLK], ACT.Tanh, scale=0.5).then_inc(gu_tanh, 1)
                act.activation(gu[:, o, 1:3, :], pb(7).rearrange("p (w n) -> p w n", w=2), ACT.Copy, scale=0.5
                               ).then_inc(gu_kept, 1)
                act.wait_ge(gu_tanh, FT * blk + m + 1 + FT * i)
                act.activation(gu[:, o, 0, :], gu[:, o, 0, :], ACT.Copy, bias=1.0).then_inc(gu_one, 1)

            def turned_maxima(g, i):
                ent = turn_entry(g)
                act.wait_ge(s_ready, ent + 1 + (2 * LSTEPS + 2) * i)
                if g > 0:
                    act.wait_ge(parts_ready, g + 2 * i)
                act.activation(neg_maxT[:, :], s_slot(ent)[0:REP * KT, 0:P], ACT.Copy).then_inc(s_done, 1)

            def gu_ahead(j):
                for m in tile_up(j):
                    keep_gu(0, m, 0)

            ahead(norm=normalise, turn=keep_turned, rope=first_part, rest=second_part, vr=keep_vr, router=router_exp,
                  comb=keep_comb, ffn=gu_ahead, maxima=lambda _: turned_maxima(0, 0))

            def keep_heads(k, i):
                act.wait_ge(pv_done, KT * (k + 1) + LSTEPS * i)
                act.wait_ge(heads_free[k % 2], 16 * REP * (k // 2 + 1) + 32 * REP * i)
                act.activation(heads[:, k % 2, :], pb(6), ACT.Copy).then_inc(pv_read, 1)

            def one(t, i):
                g, s = t // STEPS, t % STEPS
                for n in (2 * t, 2 * t + 1):
                    act.wait_ge(s_ready, pair_entry(n) + 1 + (2 * LSTEPS + 2) * i)
                    if n % 2 == 0 and n >= PSLOTS:
                        act.wait_ge(pv_done, (n - PSLOTS) // 2 + 1 + LSTEPS * i)
                    act.activation(probs[:, n % PSLOTS, :], s_slot(pair_entry(n))[:, :], ACT.Exp, scale=SCALE
                                   ).then_inc(s_done, 1)
                    if n % 2 == 0:
                        for m in tiles_up(steps_before(t, 1)):
                            keep_gu(1, m, i)
                    if n % 2 == 1 and t >= KT and t % KT == 0:
                        keep_heads(t // KT - 1, i)
                if s == STEPS - LEAD and g + 1 < G:
                    turned_maxima(g + 1, i)

            act.wait_ge(part3, ROPES)
            steps(act, one)
            keep_heads(2 * G - 1, 0)

        @block.vector
        def _(dve):
            chain = [0]

            def link(ins):
                chain[0] += 1
                ins.then_inc(vec, 1)
                dve.wait_ge(vec, chain[0])

            def block_stats(q):
                dve.wait_ge(x_in[q], 16)
                for t in range(q * TB, (q + 1) * TB):
                    last = nc.vector.bn_stats(stats[:, t, :], res[:, t, :])
                link(last)
                for t in range(q * TB, (q + 1) * TB):
                    last = nc.vector.bn_aggr(mv[:, t, :], stats[:, t, :])
                link(last)

            def norm(n):
                sl = slice(NORMS[n][0] * TB, (NORMS[n][-1] + 1) * TB)
                nc.vector.tensor_scalar(ln[:, 0, sl], mv[:, sl, 1], EPS, None, ALU.add).then_inc(var_ready, 1)
                dve.wait_ge(root_ready, n + 1)
                link(nc.vector.reciprocal(ln[:, 2, sl], ln[:, 1, sl]))
                link(nc.vector.tensor_tensor(ln[:, 3, sl], ln[:, 2, sl], ln[:, 2, sl], ALU.mult))
                link(nc.vector.tensor_tensor(ln[:, 1, sl], ln[:, 3, sl], ln[:, 0, sl], ALU.mult))
                link(nc.vector.tensor_scalar(ln[:, 3, sl], ln[:, 1, sl], -0.5, 1.5, ALU.mult, ALU.add))
                link(nc.vector.tensor_tensor(ln[:, 1, sl], ln[:, 2, sl], ln[:, 3, sl], ALU.mult))
                nc.vector.scalar_tensor_tensor(ln[:, 2, sl], mv[:, sl, 0], -1.0, ln[:, 1, sl], ALU.mult, ALU.mult
                                               ).then_inc(scale_ready, 1)

            def keep_turned(q):
                dve.wait_ge(turned, 2 * q + 2)
                nc.vector.tensor_copy(xnT[:, 1, q * BLK:(q + 1) * BLK], pb(5)).then_inc(turned_d, 1)

            def rope_products(r):
                kind, a, q = ROPE[r]
                tab = cos_sin_k[:, :, :] if kind == "k" else cos_sin[:, :, (q % QH) * BLK:(q % QH + 1) * BLK]
                if r == 0:
                    dve.wait_ge(tables_in, 16)
                if kind == "k":
                    dve.wait_ge(tables_k_in, 16)
                dve.wait_ge(qk_ready, 2 * (r + 1))
                if r >= 2:
                    dve.wait_ge(part3, r - 1)
                nc.vector.tensor_tensor(rope_a[r % 2], pb(2 * (r % 2)), tab[:, 0, :], ALU.mult).then_inc(qk_read, 1)
                nc.vector.tensor_tensor(rope_b[r % 2], pb(2 * (r % 2) + 1), tab[:, 1, :], ALU.mult
                                        ).then_inc(qk_read, 1)

            def first_rest(r):
                dve.wait_ge(part1, r + 1)
                nc.vector.tensor_tensor(rope_b[r % 2], rope_a[r % 2], parts[:, r % 2, 0, :], ALU.subtract
                                        ).then_inc(rest1, 1)

            def router(stage):
                pj = rt[:, 0, :, :].unsqueeze(2).to_broadcast((P, NT, EXP, EXP))
                pe_ = rt[:, 0, :, :].unsqueeze(3).to_broadcast((P, NT, EXP, EXP))
                if stage == 0:
                    dve.wait_ge(vr_read, 2 * NBLK)
                    link(nc.vector.tensor_reduce(rs[:, 0, :], logits[:, :, :], AX.X, ALU.max))
                    nc.vector.tensor_tensor(rt[:, 0, :, :], logits[:, :, :],
                                            rs[:, 0, :].unsqueeze(2).to_broadcast((P, NT, EXP)), ALU.subtract
                                            ).then_inc(top_max, 1)
                elif stage == 1:
                    dve.wait_ge(top_exp, 1)
                    link(nc.vector.tensor_reduce(rs[:, 0, :], rt[:, 1, :, :], AX.X, ALU.add))
                    link(nc.vector.reciprocal(rs[:, 1, :], rs[:, 0, :]))
                    link(nc.vector.tensor_tensor(rt[:, 0, :, :], rt[:, 1, :, :],
                                                 rs[:, 1, :].unsqueeze(2).to_broadcast((P, NT, EXP)), ALU.mult))
                elif stage == 2:
                    nc.vector.tensor_tensor(rank[:, 0], pj, pe_, ALU.is_gt)
                    link(nc.vector.tensor_tensor(rank[:, 1], pj, pe_, ALU.is_equal))
                elif stage == 3:
                    dve.wait_ge(before_in, 16)
                    link(nc.vector.tensor_tensor(
                        rank[:, 1], rank[:, 1],
                        before[:, :].rearrange("p (o e j) -> p o e j", o=1, e=EXP).to_broadcast((P, NT, EXP, EXP)),
                        ALU.mult))
                elif stage == 4:
                    link(nc.vector.tensor_tensor(rank[:, 0], rank[:, 0], rank[:, 1], ALU.add))
                else:
                    link(nc.vector.tensor_reduce(rt[:, 1, :, :], rank[:, 0], AX.X, ALU.add))
                    nc.vector.scalar_tensor_tensor(comb[:, :, :].rearrange("p e t -> p t e"), rt[:, 1, :, :], 2.0,
                                                   rt[:, 0, :, :], ALU.is_lt, ALU.mult).then_inc(comb_ready, 1)

            def add_down(blk, i):
                dve.wait_ge(down_done, blk + 1 + i)
                r = res[:, bass.ds((blk + i) * FTB, FTB), :].rearrange("p t e -> p (t e)")
                nc.vector.scalar_tensor_tensor(r, pb(7), 2.0, r, ALU.mult, ALU.add).then_inc(res_done, 1)

            def unit(m, i):
                g, u = m // UNITS, m % UNITS
                qt, kh, h = unit_of(u)
                if u == 0 and g >= 2:
                    dve.wait_ge(neg_ready, g - 1 + 2 * i)
                dve.wait_ge(m_ready, m + 1 + 2 * UNITS * i)
                col = (h * KT + qt) * 2 + kh
                nc.vector.tensor_reduce(unit_max[:, g % 2, col:col + 1], pb(m_bank(m)), AX.X, ALU.max
                                        ).then_inc(m_done, 1)
                if u == UNITS - 1:
                    dve.wait_ge(m_done, m + 1 + 2 * UNITS * i)
                    if g >= 1:
                        dve.wait_ge(s_ready, turn_entry(g - 1) + 1 + (2 * LSTEPS + 2) * i)
                    nc.vector.tensor_reduce(neg_max[:, g % 2, :],
                                            unit_max[:, g % 2, :].rearrange("p (c k) -> p c k", k=2), AX.X, ALU.max,
                                            negate=True).then_inc(neg_ready, 1)

            ahead(stats=block_stats, norm=norm, turn=keep_turned, rope=rope_products, rest=first_rest, router=router,
                  units=lambda m: unit(m, 0))

            def one(t, i):
                for m in range(AHEAD + UPS * t, AHEAD + UPS * (t + 1)):
                    if m < G * UNITS:
                        unit(m, i)

                p = ffn_place(t)[0]
                if t == ROT - 1:
                    add_down(0, 0)
                if p == LSTEPS - 1:
                    add_down(1, i)
                if t == INVERT_STEP:
                    dve.wait_ge(packed_in, 16)
                    nc.vector.reciprocal(packed, packed).then_inc(den_done, 1)
                for c, at in enumerate(DIVIDE_STEPS):
                    if at <= t < at + PARTS[c]:
                        divide(c, t - at)
                if PROJECT_STEP < t <= PROJECT_STEP + NT // B:
                    add_attention(t - PROJECT_STEP - 1)

            def divide(c, part):
                g0, g1, half = PIECES[c]
                places = [piece_place(k0, min(g1, k0 + 4), half) for k0 in range(g0, g1, 4)]
                if part == 0:
                    dve.wait_ge(attn_in[c], 32 * len(places))
                for a, b, rows, at in places:
                    n = (at.stop - at.start) // PARTS[c]
                    to = slice(b * S + at.start + part * n, b * S + at.start + (part + 1) * n)
                    if c > 0:
                        nc.vector.reciprocal(denT[rows, a, to], denT[rows, a, to]).then_inc(den_done, 1)
                        dve.wait_ge(den_done, 1 + sum(PARTS[1:c]) + part + 1)
                    nc.vector.tensor_tensor(attnT[rows, a, to], attnT[rows, a, to], denT[rows, a, to], ALU.mult
                                            ).then_inc(attn_done, 1)

            def add_attention(t):
                dve.wait_ge(o_ready, t + 1)
                nc.vector.tensor_tensor(res[:, t, :], out_bank(t)[:, 0:E], res[:, t, :], ALU.add).then_inc(o_done, 1)

            steps(dve, one)
            for t in range(NT // B, NT - TB):
                add_attention(t)
            for part in range(PARTS[3]):
                divide(3, part)
            for t in range(NT - TB, NT):
                add_attention(t)

        @block.tensor
        def _(pe):
            pe.wait_ge(ident_in, 16)

            def turn(q):
                pe.wait_ge(xn_ready, TB * (q + 1))
                if q >= 1:
                    pe.wait_ge(turned_a, q)
                    pe.wait_ge(turned_d, q)
                for k in range(KE):
                    for t in range(TB):
                        last = nc.tensor.transpose(pb(4 + k)[:, t * P:(t + 1) * P],
                                                   xn[:, q * TB + t, k * P:(k + 1) * P], ident[:, :])
                    last.then_inc(turned, 1)

            def project(r, rot):
                kind, a, q = ROPE[r]
                if r == 0 and rot == 0:
                    pe.wait_ge(w_qk_in, 16)
                blocks = (q + 1) if kind == "q" else QH * (a + 1)
                pe.wait_ge(turned_a, blocks)
                pe.wait_ge(turned_d, blocks)
                if r >= 2:
                    pe.wait_ge(qk_read, 2 * (r - 1))
                to = pb(2 * (r % 2) + rot)
                for k in range(KE):
                    if kind == "q":
                        last = nc.tensor.matmul(to, w_qk[:, k, rot, a * P:(a + 1) * P],
                                                xnT[:, k, q * BLK:(q + 1) * BLK], start=(k == 0), stop=(k == KE - 1))
                    else:
                        for half in range(2):
                            tok = a * S + half * BLK
                            last = nc.tensor.matmul(to[half * SH:(half + 1) * SH, :],
                                                    w_qk[:, k, rot, 2 * P:2 * P + SH], xnT[:, k, tok:tok + BLK],
                                                    start=(k == 0), stop=(k == KE - 1))
                last.then_inc(qk_ready, 1)

            def values_router(q):
                pe.wait_ge(turned_a, q + 1)
                pe.wait_ge(turned_d, q + 1)
                if q == 0:
                    pe.wait_ge(w_vr_in, 16)
                if q >= 2:
                    pe.wait_ge(vr_read, 2 * (q if q == 3 else q - 1))
                C = KV * D + EXP
                for t in range(TB):
                    for k in range(KE):
                        last = nc.tensor.matmul(vr_bank(q)[:, t * C:(t + 1) * C],
                                                xnT[:, k, q * BLK + t * P:q * BLK + (t + 1) * P],
                                                w_vr[:, k, :], start=(k == 0), stop=(k == KE - 1))
                last.then_inc(vr_ready, 1)

            def turn_comb(_):
                pe.wait_ge(comb_ready, 1)
                pe.wait_ge(vr_read, 2 * NBLK)
                pe.wait_ge(m_done, UNITS_AT_COMB)
                nc.tensor.transpose(pb(6)[:, 0:P], comb[:, :, :].rearrange("p e t -> p (e t)"), ident[:, :]
                                    ).then_inc(comb_turned, 1)

            def feed_forward(blk, j, i):
                if j < UP_MM * FT:
                    m, w, k = j // UP_MM, j % UP_MM // KE, j % KE
                    if m == 0 and j == 0:
                        if blk == 0:
                            pe.wait_ge(w_gu_in, 16)
                            pe.wait_ge(vr_read, 2 * NBLK)
                        else:
                            pe.wait_ge(res_done, blk + i)
                    elif j % UP_MM == 0:
                        pe.wait_ge(gu_tanh, FT * blk + m + FT * i)
                        pe.wait_ge(gu_kept, FT * blk + m + FT * i)
                    mm = nc.tensor.matmul(pb(7)[:, w * FBLK:(w + 1) * FBLK], w_gu[:, k, m, w, :],
                                          xnT[:, k, bass.ds((blk + i) * FBLK, FBLK)], start=(k == 0), stop=(k == KE - 1))
                    if j % UP_MM == UP_MM - 1:
                        mm.then_inc(gu_ready, 1)
                elif j >= DOWN_AT:
                    tt, m = (j - DOWN_AT) // FT, (j - DOWN_AT) % FT
                    if j == DOWN_AT:
                        if blk == 0:
                            pe.wait_ge(w_dn_in, 16)
                        pe.wait_ge(gu_tanh, FT * (blk + 1) + FT * i)
                        pe.wait_ge(gu_kept, FT * (blk + 1) + FT * i)
                    if tt == 0:
                        pe.wait_ge(hid_steps, HID * blk + hid_count(m + 1) + HID * i)
                    mm = nc.tensor.matmul(pb(7)[:, tt * E:(tt + 1) * E], hid[:, m, tt * P:(tt + 1) * P],
                                          w_dn[:, m, :], start=(m == 0), stop=(m == FT - 1))
                    if j == SLOTS - 1:
                        mm.then_inc(down_done, 1)

            def unit(m, i):
                g, u = m // UNITS, m % UNITS
                qt, kh, h = unit_of(u)
                n = g % 2
                if u == 0:
                    pe.wait_ge(qk1_in[n], 64 * (g // 2 + 1) + 64 * i)
                if m >= 3:
                    pe.wait_ge(m_done, m - (2 if m < THREE else 1) + 2 * UNITS * i)
                elif m == 2:
                    pe.wait_ge(vr_read, 4)
                else:
                    pe.wait_ge(turned_a, NBLK)
                    pe.wait_ge(turned_d, NBLK)
                if UNITS_AT_COMB <= m < UNITS_AT_COMB + 3 and m_bank(m) == 6:
                    pe.wait_ge(comb_kept, 1)
                rows = slice(SH * (h % 2), SH * (h % 2) + SH)
                nc.tensor.matmul(pb(m_bank(m)), q1[rows, n, h // 2, qt * P:(qt + 1) * P],
                                 k1[rows, n, kh * BLK:(kh + 1) * BLK], start=True, stop=True).then_inc(m_ready, 1)

            def turn_maxima(g, i):
                ent = turn_entry(g)
                pe.wait_ge(neg_ready, g + 1 + 2 * i)
                if ent >= 2:
                    pe.wait_ge(s_done, ent - 1 + (2 * LSTEPS + 2) * i)
                nc.tensor.transpose(s_slot(ent)[0:REP * KT, 0:P], neg_max[:, g % 2, :], ident[:, :]
                                    ).then_inc(s_ready, 1)

            def scores(n, i):
                g, s = n // 2 // STEPS, n // 2 % STEPS
                qh, kt = s // KT, s % KT
                e = pair_entry(n)
                if e >= 2:
                    pe.wait_ge(s_done, e - 1 + (2 * LSTEPS + 2) * i)
                for h in range(2):
                    rows = slice(SH * h, SH * h + SH)
                    last = nc.tensor.matmul(s_slot(e)[:, h * BLK:(h + 1) * BLK], k2[rows, g % 2, kt * P:(kt + 1) * P],
                                            q2[rows, g % 2, n % 2, qh * BLK:(qh + 1) * BLK], start=True, stop=True)
                last.then_inc(s_ready, 1)

            def weigh_values(t, i):
                g, kt, k = t // STEPS, t % KT, t // KT
                if kt == 0 and k >= 1:
                    pe.wait_ge(pv_read, k + 4 * i)
                if t % STEPS == 0:
                    pe.wait_ge(v_ready, g + 1 + 2 * i)
                pe.wait_ge(s_done, pair_entry(2 * t + 1) + 1 + (2 * LSTEPS + 2) * i)
                for h in range(REP):
                    n = 2 * t + h // 2
                    last = nc.tensor.matmul(pb(6)[32 * h:32 * h + 32, :], v_now[:, g % 2, kt, :],
                                            probs[:, n % PSLOTS, (h % 2) * BLK:(h % 2 + 1) * BLK],
                                            start=(kt == 0), stop=(kt == KT - 1))
                last.then_inc(pv_done, 1)

            def first_maxima(_):
                pe.wait_ge(qk_read, 2 * ROPES)
                turn_maxima(0, 0)

            def project_out(t):
                for a in range(KE):
                    last = nc.tensor.matmul(out_bank(t)[:, 0:E], attnT[:, a, t * P:(t + 1) * P], w_o[:, a, :],
                                            start=(a == 0), stop=(a == KE - 1))
                last.then_inc(o_ready, 1)

            ahead(turn=turn, plain=lambda r: project(r, 0), other=lambda r: project(r, 1), vr=values_router,
                  comb=turn_comb, units=lambda m: unit(m, 0), ffn=lambda j: feed_forward(0, j, 0), maxima=first_maxima)
            pe.wait_ge(comb_kept, 1)

            def one(t, i):
                g, s = t // STEPS, t % STEPS
                if s == 0:
                    pe.wait_ge(qk2_in[g % 2], 64 * (g // 2 + 1) + 64 * i)
                    pe.wait_ge(rows_in[g % 2], 32 * (g // 2 + 1) + 32 * i)
                scores(2 * t, i)
                scores(2 * t + 1, i)
                for n in range(2):
                    for m in range(AHEAD + UPS * t + 2 * n, AHEAD + UPS * t + 2 * n + 2):
                        if m < G * UNITS:
                            unit(m, i)
                    if n == 0 and t >= 1:
                        weigh_values(t - 1, i)
                    if t < ROT:
                        feed_forward(0, SLOTS - 2 * ROT + 2 * t + n, 0)
                    for j in ffn_place(t)[1][n:1 + 2 * n]:
                        feed_forward(1, j, i)
                if s == STEPS - LEAD and g + 1 < G:
                    turn_maxima(g + 1, i)
                if PROJECT_STEP <= t < PROJECT_STEP + NT // B:
                    o = t - PROJECT_STEP
                    if o == 0:
                        pe.wait_ge(w_o_in, 16)
                        pe.wait_ge(attn_done, 2)
                        pe.wait_ge(res_done, TURNS + 1)
                        pe.wait_ge(m_done, G * UNITS)
                    if o >= 2:
                        pe.wait_ge(o_done, o - 1)
                    project_out(o)

            steps(pe, one)
            weigh_values(G * STEPS - 1, 0)

            pe.wait_ge(pv_read, 2 * G)
            pe.wait_ge(o_done, NT // B)
            pe.wait_ge(s_done, entries(G * STEPS))
            for t in range(NT // B, NT):
                pe.wait_ge(attn_done, 3 + sum(PARTS[1:3]) + max(t - (NT - TB) + 1, 0))
                project_out(t)


def kernel(L0_attn_x, L0_attn_Wq, L0_attn_Wk, L0_attn_Wv, L0_attn_Wo, L0_ffn_router_w, L0_ffn_shared_gate,
           L0_ffn_shared_up, L0_ffn_shared_down, L0_ffn_w_gate, L0_ffn_w_up, L0_ffn_w_down):
    import concourse.bacc as bacc
    from concourse.bass_utils import run_bass_kernel_spmd

    def a(v):
        return np.asarray(v)

    order = np.arange(E).reshape(KV, 2, 2, D).transpose(0, 2, 3, 1).reshape(-1)
    swap = np.arange(E).reshape(-1, 2, HALF)[:, ::-1].reshape(-1)
    wq, wk, wv = a(L0_attn_Wq), a(L0_attn_Wk), a(L0_attn_Wv)
    plain = np.concatenate([wq[order], wk])
    other = np.concatenate([wq[swap[order]], wk[swap[:KV * D]]])
    wqkv = np.stack([plain.T, other.T], 1).reshape(KE, P, 2, -1).transpose(1, 0, 2, 3)
    wvr = np.concatenate([wv.T, a(L0_ffn_router_w)], 1).reshape(KE, P, -1).transpose(1, 0, 2)
    wo = a(L0_attn_Wo).T.reshape(KE, P, E).transpose(1, 0, 2)
    sg, su, eg, eu = a(L0_ffn_shared_gate), a(L0_ffn_shared_up), a(L0_ffn_w_gate), a(L0_ffn_w_up)
    gate = np.concatenate([sg, eg.transpose(1, 0, 2).reshape(E, -1)], 1).reshape(E, FT, P)
    up = np.concatenate([su, eu.transpose(1, 0, 2).reshape(E, -1)], 1).reshape(E, FT, P)
    wgu = np.stack([gate, up], 2).reshape(KE, P, FT, 2, P).transpose(1, 0, 2, 3, 4)
    wdn = np.concatenate([a(L0_ffn_shared_down).reshape(2, P, E), a(L0_ffn_w_down)]).transpose(1, 0, 2)

    f = np.float32
    inv = (f(1.0) / np.power(f(10000.0), np.arange(0, D, 2, dtype=f) / f(D))).astype(f)
    angle = np.outer(np.arange(S, dtype=f), inv).astype(f)

    def rotation(dim):
        sign = np.where(dim < HALF, f(-1), f(1))[:, None]
        return np.cos(angle).T[dim % HALF], np.sin(angle).T[dim % HALF] * sign

    before = np.broadcast_to(np.tril(np.ones((EXP, EXP), f), -1).reshape(1, -1), (P, EXP * EXP))
    stack = [np.concatenate([v[:SH, :BLK], v[:SH, BLK:]]) for v in rotation(np.arange(P) % D)]
    tables = np.concatenate([np.eye(P, dtype=f), before, *rotation(order[:P] % D), *stack], 1).astype(f)

    arrays = {"x": a(L0_attn_x).reshape(N, E), "wqkv": wqkv, "wo": wo, "wgu": wgu, "wdn": wdn, "wvr": wvr,
              "tables": tables}
    arrays = {k: np.ascontiguousarray(v) for k, v in arrays.items()}
    nc = bacc.Bacc("TRN2", target_bir_lowering=False, num_devices=1)
    aps = {k: nc.dram_tensor(k, v.shape, mybir.dt.from_np(v.dtype), kind="ExternalInput").ap()
           for k, v in arrays.items()}
    out = nc.dram_tensor("out", (N, E), F32, kind="ExternalOutput").ap()
    ffn_attention_block(nc, out=out, **aps)
    r = run_bass_kernel_spmd(nc, [arrays], core_ids=[0])
    return r.results[0]["out"].reshape(B, S, E)
```
